# Optimizing a Trainium2 kernel written in Bass

```python
import numpy as np
import jax
import jax.numpy as jnp

def _softmax(x, axis=-1):
    return jax.nn.softmax(x, axis=axis)

def _gelu(x):
    return jax.nn.gelu(x, approximate=True)

def _silu(x):
    return jax.nn.silu(x)

def _sigmoid(x):
    return jax.nn.sigmoid(x)

def _layernorm(x, axis=-1, eps=1e-05):
    m = jnp.mean(x, axis=axis, keepdims=True)
    v = jnp.var(x, axis=axis, keepdims=True)
    return (x - m) / jnp.sqrt(v + eps)

def _scatter_add(tgt, idx, src, axis=0):
    return tgt.at[idx].add(src)

def _segment_sum(src, seg, n):
    return jax.ops.segment_sum(src, seg, n)
kernel_name = 'mk_adj_resnorm_d4_adj_r2_747320'

def setup_inputs(seed: int=0):
    np.random.seed(seed)
    _w = jnp.asarray

    def _rec_inputs():
        import jax
        import jax.numpy as jnp
        _gk = jax.random.key(seed)
        x = -0.0005207 + 1.001 * jax.random.normal(jax.random.fold_in(_gk, 1), (128, 128, 128), jnp.float32)
        _a = jax.random.bernoulli(jax.random.fold_in(_gk, 2), 0.125, (128, 128, 128))
        _a = jnp.logical_or(_a, jnp.swapaxes(_a, -1, -2))
        _a = jnp.logical_or(_a, jnp.eye(128, dtype=bool))
        adj = _a.astype(jnp.int32)
        _nm = jnp.ones((128, 128), dtype=bool)
        nodemask = jnp.where(_nm, 1.0, 0.0).astype(jnp.float32)
        return (x, adj, nodemask)
    x, adj, nodemask = _rec_inputs()

    def _L0_gnn_setup():
        import jax, jax.numpy as jnp
        import numpy as np
        B, N, D_IN, D_OUT, H = (8, 512, 128, 128, 8)
        HD = D_OUT // H
        ALPHA = 0.2
        key = jax.random.key(seed)
        k1, k2, k3, k4 = jax.random.split(key, 4)
        h = jax.random.normal(k1, (B, N, D_IN), dtype=jnp.float32)
        adj_mask = jax.random.randint(k2, (B, N, N), 0, 2, dtype=jnp.int64)
        idx = jnp.arange(N)
        adj_mask = adj_mask.at[:, idx, idx].set(1)
        lim_W = float(np.sqrt(6.0 / (D_IN + D_OUT)))
        W = jax.random.uniform(k3, (D_IN, D_OUT), minval=-lim_W, maxval=lim_W, dtype=jnp.float32)
        lim_a = float(np.sqrt(6.0 / (2 * HD + 1)))
        a = jax.random.uniform(k4, (2 * HD,), minval=-lim_a, maxval=lim_a, dtype=jnp.float32)
        return {'h': h, 'adj_mask': adj_mask, 'W': W, 'a': a}
    _L0_gnn_all = _L0_gnn_setup()
    _L0_gnn_in = {k: v for k, v in _L0_gnn_all.items() if k in ('W', 'a')}
    del _L0_gnn_all

    def _L1_gnn_setup():
        import jax, jax.numpy as jnp
        import numpy as np
        NEG_BIG = -9000000000000000.0
        LEAKY_SLOPE = 0.2
        key = jax.random.key(seed)
        k1, k2, k3, k4 = jax.random.split(key, 4)
        B, N, F_in, F_out = (8, 1024, 128, 128)
        h = jax.random.normal(k1, (B, N, F_in), dtype=jnp.float32)
        adj = jax.random.randint(k2, (B, N, N), 0, 2, dtype=jnp.int32)
        W = jax.random.normal(k3, (F_out, F_in), dtype=jnp.float32) * (1.414 * (6.0 / (F_in + F_out)) ** 0.5)
        a = jax.random.normal(k4, (2 * F_out, 1), dtype=jnp.float32) * 0.1
        return {'h': h, 'adj': adj, 'W': W, 'a': a}
    _L1_gnn_all = _L1_gnn_setup()
    _L1_gnn_in = {k: v for k, v in _L1_gnn_all.items() if k in ('W', 'a')}
    del _L1_gnn_all

    def _L2_gnn_setup():
        import jax, jax.numpy as jnp
        import numpy as np
        D_MODEL = 128
        NUM_REL = 40

        def _direction(x, W, Wg, b, bg, adj, rel_ids):
            h = x @ W.T
            g = h @ Wg.T
            vals = (h[:, :, None, :] + b) * jax.nn.sigmoid(g[:, :, None, :] + bg)
            onehot = (adj[..., None] == rel_ids).astype(h.dtype)
            return jnp.einsum('bnmr,bmrd->bnd', onehot, vals)
        key = jax.random.key(seed)
        ks = jax.random.split(key, 16)
        B, N, d = (2, 256, D_MODEL)
        s = 0.02
        inp = {'node': jax.random.normal(ks[0], (B, N, d), dtype=jnp.float32), 'node_mask': jnp.ones((B, N), dtype=jnp.float32), 'adj_mat': jax.random.randint(ks[1], (B, N, N), 0, 41, dtype=jnp.int32), 'W_fwd': jax.random.normal(ks[2], (d, d), dtype=jnp.float32) * s, 'W_bwd': jax.random.normal(ks[3], (d, d), dtype=jnp.float32) * s, 'W_loop': jax.random.normal(ks[4], (d, d), dtype=jnp.float32) * s, 'Wg_fwd': jax.random.normal(ks[5], (d, d), dtype=jnp.float32) * s, 'Wg_bwd': jax.random.normal(ks[6], (d, d), dtype=jnp.float32) * s, 'Wg_loop': jax.random.normal(ks[7], (d, d), dtype=jnp.float32) * s, 'b_fwd': jax.random.normal(ks[8], (NUM_REL - 1, d), dtype=jnp.float32) * s, 'b_bwd': jax.random.normal(ks[9], (NUM_REL - 1, d), dtype=jnp.float32) * s, 'b_loop': jax.random.normal(ks[10], (1, d), dtype=jnp.float32) * s, 'bg_fwd': jax.random.normal(ks[11], (NUM_REL - 1, d), dtype=jnp.float32) * s, 'bg_bwd': jax.random.normal(ks[12], (NUM_REL - 1, d), dtype=jnp.float32) * s, 'bg_loop': jax.random.normal(ks[13], (1, d), dtype=jnp.float32) * s}
        return inp
    _L2_gnn_all = _L2_gnn_setup()
    _L2_gnn_in = {k: v for k, v in _L2_gnn_all.items() if k in ('W_fwd', 'W_bwd', 'W_loop', 'Wg_fwd', 'Wg_bwd', 'Wg_loop', 'b_fwd', 'b_bwd', 'b_loop', 'bg_fwd', 'bg_bwd', 'bg_loop')}
    del _L2_gnn_all

    def _L3_gnn_setup():
        import jax, jax.numpy as jnp
        import numpy as np
        B, N, E, H = (2, 1024, 128, 4)
        DK = E // H
        key = jax.random.key(seed)
        ks = jax.random.split(key, 7)
        xav = lambda k, shape, fan_in, fan_out: jax.random.uniform(k, shape, minval=-1.0, maxval=1.0, dtype=jnp.float32) * np.sqrt(6.0 / (fan_in + fan_out))
        return {'node_embeddings': jax.random.normal(ks[0], (B, N, E), dtype=jnp.float32), 'adjacency_matrices': jax.random.randint(ks[1], (B, N, N), 0, 2, dtype=jnp.int32), 'Wq': xav(ks[2], (H, E, DK), E, DK), 'Wk': xav(ks[3], (H, E, DK), E, DK), 'Wv': xav(ks[4], (H, E, DK), E, DK), 'Wo': xav(ks[5], (E, E), E, E), 'bo': jnp.zeros((E,), dtype=jnp.float32)}
    _L3_gnn_all = _L3_gnn_setup()
    _L3_gnn_in = {k: v for k, v in _L3_gnn_all.items() if k in ('Wq', 'Wk', 'Wv', 'Wo', 'bo')}
    del _L3_gnn_all
    return {'x': x, 'adj': adj, 'nodemask': nodemask, 'L0_gnn_W': _L0_gnn_in['W'], 'L0_gnn_a': _L0_gnn_in['a'], 'L1_gnn_W': _L1_gnn_in['W'], 'L1_gnn_a': _L1_gnn_in['a'], 'L2_gnn_W_fwd': _L2_gnn_in['W_fwd'], 'L2_gnn_W_bwd': _L2_gnn_in['W_bwd'], 'L2_gnn_W_loop': _L2_gnn_in['W_loop'], 'L2_gnn_Wg_fwd': _L2_gnn_in['Wg_fwd'], 'L2_gnn_Wg_bwd': _L2_gnn_in['Wg_bwd'], 'L2_gnn_Wg_loop': _L2_gnn_in['Wg_loop'], 'L2_gnn_b_fwd': _L2_gnn_in['b_fwd'], 'L2_gnn_b_bwd': _L2_gnn_in['b_bwd'], 'L2_gnn_b_loop': _L2_gnn_in['b_loop'], 'L2_gnn_bg_fwd': _L2_gnn_in['bg_fwd'], 'L2_gnn_bg_bwd': _L2_gnn_in['bg_bwd'], 'L2_gnn_bg_loop': _L2_gnn_in['bg_loop'], 'L3_gnn_Wq': _L3_gnn_in['Wq'], 'L3_gnn_Wk': _L3_gnn_in['Wk'], 'L3_gnn_Wv': _L3_gnn_in['Wv'], 'L3_gnn_Wo': _L3_gnn_in['Wo'], 'L3_gnn_bo': _L3_gnn_in['bo']}

def reference(x, adj, nodemask, L0_gnn_W, L0_gnn_a, L1_gnn_W, L1_gnn_a, L2_gnn_W_fwd, L2_gnn_W_bwd, L2_gnn_W_loop, L2_gnn_Wg_fwd, L2_gnn_Wg_bwd, L2_gnn_Wg_loop, L2_gnn_b_fwd, L2_gnn_b_bwd, L2_gnn_b_loop, L2_gnn_bg_fwd, L2_gnn_bg_bwd, L2_gnn_bg_loop, L3_gnn_Wq, L3_gnn_Wk, L3_gnn_Wv, L3_gnn_Wo, L3_gnn_bo):
    import jax
    import jax.numpy as jnp

    def _L0_gnn_ref(h, adj_mask, W, a):
        import jax, jax.numpy as jnp
        import numpy as np
        B, N, D_IN, D_OUT, H = (8, 512, 128, 128, 8)
        HD = D_OUT // H
        ALPHA = 0.2
        b, n, _ = h.shape
        Wh = (h @ W).reshape(b, n, H, HD).transpose(0, 2, 1, 3)
        a1, a2 = (a[:HD], a[HD:])
        e1 = jnp.einsum('bhnd,d->bhn', Wh, a1)
        e2 = jnp.einsum('bhnd,d->bhn', Wh, a2)
        e = e1[:, :, :, None] + e2[:, :, None, :]
        mask = adj_mask[:, None, :, :] == 0
        e = jnp.where(mask, -jnp.inf, e)
        e = jnp.where(e >= 0, e, ALPHA * e)
        attn = jax.nn.softmax(e, axis=-1)
        h_prime = jnp.einsum('bhij,bhjd->bhid', attn, Wh)
        return h_prime.transpose(0, 2, 1, 3).reshape(b, n, D_OUT)

    def _L1_gnn_ref(h, adj, W, a):
        import jax, jax.numpy as jnp
        import numpy as np
        NEG_BIG = -9000000000000000.0
        LEAKY_SLOPE = 0.2
        Wh = jnp.einsum('bnf,of->bno', h, W)
        F_out = W.shape[0]
        a1 = a[:F_out, 0]
        a2 = a[F_out:, 0]
        s1 = Wh @ a1
        s2 = Wh @ a2
        e = s1[:, :, None] + s2[:, None, :]
        e = jax.nn.leaky_relu(e, negative_slope=LEAKY_SLOPE)
        e = jnp.where(adj == 0, NEG_BIG, e)
        attention = jax.nn.softmax(e, axis=-1)
        h_prime = jnp.einsum('bij,bjf->bif', attention, Wh)
        return jax.nn.elu(h_prime)

    def _L2_gnn_ref(node, node_mask, adj_mat, W_fwd, W_bwd, W_loop, Wg_fwd, Wg_bwd, Wg_loop, b_fwd, b_bwd, b_loop, bg_fwd, bg_bwd, bg_loop):
        import jax, jax.numpy as jnp
        import numpy as np
        D_MODEL = 128
        NUM_REL = 40

        def _direction(x, W, Wg, b, bg, adj, rel_ids):
            h = x @ W.T
            g = h @ Wg.T
            vals = (h[:, :, None, :] + b) * jax.nn.sigmoid(g[:, :, None, :] + bg)
            onehot = (adj[..., None] == rel_ids).astype(h.dtype)
            return jnp.einsum('bnmr,bmrd->bnd', onehot, vals)
        rels = jnp.arange(2, NUM_REL + 1, dtype=adj_mat.dtype)
        rel1 = jnp.array([1], dtype=adj_mat.dtype)
        adj_t = jnp.swapaxes(adj_mat, -1, -2)
        out = _direction(node, W_fwd, Wg_fwd, b_fwd, bg_fwd, adj_mat, rels)
        out = out + _direction(node, W_bwd, Wg_bwd, b_bwd, bg_bwd, adj_t, rels)
        out = out + _direction(node, W_loop, Wg_loop, b_loop, bg_loop, adj_t, rel1)
        return jax.nn.relu(out)

    def _L3_gnn_ref(node_embeddings, adjacency_matrices, Wq, Wk, Wv, Wo, bo):
        import jax, jax.numpy as jnp
        import numpy as np
        B, N, E, H = (2, 1024, 128, 4)
        DK = E // H
        Q = jnp.einsum('bnd,hde->bhne', node_embeddings, Wq)
        K = jnp.einsum('bnd,hde->bhne', node_embeddings, Wk)
        V = jnp.einsum('bnd,hde->bhne', node_embeddings, Wv)
        scale = 1.0 / np.sqrt(DK).astype(np.float32)
        scores = jnp.einsum('bhne,bhme->bhnm', Q, K) * scale
        mask = adjacency_matrices[:, None, :, :] > 0
        scores = jnp.where(mask, scores, -jnp.inf)
        attn = jax.nn.softmax(scores, axis=-1)
        heads = jnp.einsum('bhnm,bhme->bhne', attn, V)
        concat = heads.transpose(0, 2, 1, 3).reshape(node_embeddings.shape[0], node_embeddings.shape[1], E)
        return concat @ Wo.T + bo
    x = _layernorm(x + _L0_gnn_ref(x, adj, L0_gnn_W, L0_gnn_a), axis=-1)
    x = _layernorm(x + _L1_gnn_ref(x, adj, L1_gnn_W, L1_gnn_a), axis=-1)
    x = _layernorm(x + _L2_gnn_ref(x, nodemask, adj, L2_gnn_W_fwd, L2_gnn_W_bwd, L2_gnn_W_loop, L2_gnn_Wg_fwd, L2_gnn_Wg_bwd, L2_gnn_Wg_loop, L2_gnn_b_fwd, L2_gnn_b_bwd, L2_gnn_b_loop, L2_gnn_bg_fwd, L2_gnn_bg_bwd, L2_gnn_bg_loop), axis=-1)
    x = _layernorm(x + _L3_gnn_ref(x, adj, L3_gnn_Wq, L3_gnn_Wk, L3_gnn_Wv, L3_gnn_Wo, L3_gnn_bo), axis=-1)
    return x

_drawn_inputs = setup_inputs


def setup_inputs(seed=0):
    import zlib

    import numpy as np

    out = dict(_drawn_inputs(seed))
    spreads = {'L3_gnn_bo': (0.0, 0.1)}
    factors = {'L2_gnn_Wg_loop': 3.82, 'L2_gnn_bg_loop': 5.678}
    for name, (base, spread) in spreads.items():
        noise = np.random.default_rng([zlib.crc32(name.encode()), seed]).standard_normal(out[name].shape)
        drawn = base * np.exp(spread * noise) if base else spread * noise
        out[name] = jnp.asarray(drawn.astype(out[name].dtype))
    for name, factor in factors.items():
        out[name] = (out[name] * factor).astype(out[name].dtype)
    return out
```

```python
import concourse.bass as bass
from concourse import mybir
from contextlib import ExitStack

F32 = mybir.dt.float32
BF16 = mybir.dt.bfloat16
I32 = mybir.dt.int32
ALU = mybir.AluOpType
ACT = mybir.ActivationFunctionType
AX_X = mybir.AxisListType.X

B = 128
N = 128
D = 128
EPS = 1e-5
NG = 4
T = B // NG
RING = 4
BANK = 512
LOOP0, LOOP1 = 2, 30


def need(eng, sem, value):
    if isinstance(value, int) and value <= 0:
        return
    eng.wait_ge(sem, value)


def steps(eng, body, first=0):
    for t in range(first, LOOP0):
        body(t, t % RING, t // RING)
    with eng.Fori(0, (LOOP1 - LOOP0) // RING) as i:
        for r in range(RING):
            s = LOOP0 + r
            body(i * RING + s, s % RING, i + s // RING)
    for t in range(LOOP1, T):
        body(t, t % RING, t // RING)


def known(t):
    return isinstance(t, int)


def constants(nc, tsb, sem, sb, pb, c, k):
    k["ident"] = sb("ident", [N, N], F32)
    k["eye3"] = sb("eye3", [96, 32], BF16)
    k["sel"] = sb("sel", [96, 32, N], BF16)
    k["ones96"] = sb("ones96", [96, N], BF16)
    k["onescol"] = sb("onescol", [N, 1], F32)
    k["onesf"] = sb("onesf", [32, N], F32)
    k["minushalf"] = sb("minushalf", [N, 1], F32)
    k["headsum"] = sb("headsum", [N, N], BF16)
    for n, w in (("w0", D), ("w1t", D), ("w3q", D), ("w3k", D), ("w3v", D), ("w3ot", D)):
        k[n] = sb(n, [D, w], F32)
    k["wa0"] = sb("wa0", [D, 16], F32)
    k["wa1"] = sb("wa1", [D, 2], F32)
    k["w2"] = sb("w2", [D, 2 * D], F32)
    k["bias2"] = sb("bias2", [96, 2 * D], BF16)
    k["bias3"] = sb("bias3", [96, D], BF16)
    if True:
        def tb(n, s, d=F32):
            return tsb(n, s, d)
        w0t, w1, wl, wlt, wgt = (tb(n, [D, D]) for n in ("w0t", "w1_", "wl", "wlt", "wgt"))
        a0c = tb("a0c", [D, 2])
        a0blk = tb("a0blk", [D, 2, 8])
        hb = tb("hb", [D, 8])
        a1c = tb("a1c", [D, 2])
        brow = tb("brow", [96, 3 * D])
        bres = tb("bres", [96, 3 * D])
        ball = tb("ball", [96, 3 * D], BF16)
        loaded, cast, zeroed, made, mult = (sem(f"const_{n}") for n in ("loaded", "cast", "zeroed", "made", "mult"))
        rowed = sem("const_rowed")
        loads = [(k["ident"], c["ident"]), (k["w0"], c["w0"]), (w0t, c["w0t"]), (w1, c["w1"]), (k["w1t"], c["w1t"]),
                 (wl, c["wl"]), (wlt, c["wlt"]), (wgt, c["wgt"]), (k["w3q"], c["wq"]), (k["w3k"], c["wk"]),
                 (k["w3v"], c["wv"]), (k["w3ot"], c["wot"]), (a0c, c["a0"]), (hb, c["hb"]), (a1c, c["a1"])]
        casts = [(k["eye3"], c["eye3"]), (k["headsum"], c["headsum"])]
        rows = 0
        with nc.Block() as block:
            @block.sync
            def _(sp):
                for dst, src in loads:
                    sp.dma_start(dst[:, :], src).then_inc(loaded, 16)
                sp.wait_ge(zeroed, 1)
                for q in range(3):
                    for n, src in enumerate((c["b2"], c["bg2"], c["bo"])):
                        sp.dma_start(brow[32 * q:32 * q + 1, n * D:(n + 1) * D], src).then_inc(rowed, 16)

            @block.gpsimd
            def _(pool):
                for dst, src in casts:
                    pool.dma_start(dst[:, :], src).then_inc(cast, 16)

            @block.vector
            def _(dve):
                nc.vector.memset(brow[:, :], 0.0).then_inc(zeroed, 1)
                nc.vector.memset(k["ones96"][:, :], 1.0)
                nc.vector.memset(k["minushalf"][:, :], -0.5)
                nc.vector.memset(k["onesf"][:, :], 1.0)
                nc.vector.memset(k["onescol"][:, :], 1.0)
                dve.wait_ge(cast, 16 * len(casts))
                nc.vector.tensor_copy(k["sel"][:, :, :], k["eye3"][:, :].rearrange("p (r o) -> p r o", o=1).to_broadcast([96, 32, N]))
                dve.wait_ge(loaded, 16 * len(loads))
                for e in range(2):
                    ins = nc.vector.tensor_scalar(a0blk[:, e, :], hb[:, :], a0c[:, e:e + 1], None, ALU.mult)
                ins.then_inc(made, 1)
                dve.wait_ge(rowed, 16 * 9)
                dve.wait_ge(zeroed, 1)
                nc.vector.tensor_scalar(brow[:, 0:D], brow[:, 0:D], 0.5, None, ALU.mult).then_inc(made, 1)
                dve.wait_ge(made, 2)
                nc.vector.tensor_copy(ball[:, :], brow[:, :]).then_inc(made, 1)
                dve.wait_ge(made, 3)
                nc.vector.tensor_tensor(bres[0:64, :], brow[0:64, :], ball[0:64, :], ALU.subtract).then_inc(made, 1)
                dve.wait_ge(made, 4)
                nc.vector.tensor_copy(ball[0:64, :], bres[0:64, :]).then_inc(made, 1)
                dve.wait_ge(made, 5)
                nc.vector.tensor_tensor(ball[0:32, :], bres[0:32, :], ball[0:32, :], ALU.subtract).then_inc(made, 1)
                dve.wait_ge(made, 6)
                nc.vector.tensor_copy(k["bias2"][:, :], ball[:, 0:2 * D])
                nc.vector.tensor_copy(k["bias3"][:, :], ball[:, 2 * D:])
                nc.vector.tensor_scalar(k["w2"][:, 0:D], wlt[:, :], 0.5, None, ALU.mult)
                dve.wait_ge(mult, 1)
                nc.vector.tensor_copy(k["wa0"][:, :], pb[0][:, 0:16])
                nc.vector.tensor_copy(k["wa1"][:, :], pb[0][:, 16:18])
                nc.vector.tensor_copy(k["w2"][:, D:2 * D], pb[0][:, D:2 * D])

            @block.tensor
            def _(pe):
                pe.wait_ge(loaded, 16 * len(loads))
                pe.wait_ge(made, 1)
                nc.tensor.matmul(pb[0][:, 0:16], w0t[:, :], a0blk[:, :, :].rearrange("p e h -> p (e h)"), start=True, stop=True)
                nc.tensor.matmul(pb[0][:, 16:18], w1[:, :], a1c[:, :], start=True, stop=True)
                nc.tensor.matmul(pb[0][:, D:2 * D], wl[:, :], wgt[:, :], start=True, stop=True).then_inc(mult, 1)


def gat(nc, sb, sem, pb, k, L, heads, yres, stats, mean, rstd, dmin, x_ngd, xt_dgn, adjt):
    H, hd = heads, D // heads
    w = hd + 1
    kin = H * w
    U = 4 if H > 1 else 1
    gpu = NG // U
    R = NG * H
    first = L == 0
    wa = k["wa0"] if first else k["wa1"]
    wm = k["w0"] if first else k["w1t"]

    if first:
        S = [pb.pair(0), pb.pair(2)]
    else:
        S = [pb[0], pb[2]]
    PT = pb[1]
    Q = [pb[4], pb[5]]
    W, E = pb[6], pb[7]
    e_ps = E[:, 0:2 * R].rearrange("p (k r) -> p k r", k=2)
    m_ps = E[:, 448:448 + R]
    t_ps = E[0:96, 128:128 + 2 * N].rearrange("p (k n) -> p k n", k=2)

    xr = sb(f"x{L}", [N, RING, NG, D], F32)
    xt = sb(f"xt{L}", [D, RING, NG, N], F32)
    adj = sb(f"adj{L}", [N, RING, NG, N], BF16)
    nota = sb(f"nota{L}", [N, RING, NG, N], BF16)
    nega = sb(f"nega{L}", [N, RING, NG, N], BF16)
    erep = sb(f"erep{L}", [N, 2, 2, 3, 32], F32)
    rmax = sb(f"rmax{L}", [32, 1], F32)
    rdiag = sb(f"rdiag{L}", [32, R], F32)
    arg = sb(f"arg{L}", [N, 4, R], F32)
    cc = sb(f"cc{L}", [N, R], F32)
    vu = sb(f"vu{L}", [N, RING, 4, R], F32)
    yy = sb(f"yy{L}", [N, 2, NG, 2, H, w], F32)
    yrest = sb(f"yrest{L}", [N, 2, NG * 2 * kin], F32)
    yp = [sb(f"y{p}{L}", [N, RING, NG, 2, H, w], BF16) for p in ("hi", "mid", "lo")]
    rows = sb(f"rows{L}", [96, 2, 2, N], BF16)
    rrest = sb(f"rrest{L}", [64, 2, N], F32)
    sg = sb(f"sg{L}", [N, 2, BANK * (2 if first else 1)], BF16)
    pos = sb(f"pos{L}", [N, 2, BANK * (2 if first else 1)], BF16)
    tt = sb(f"tt{L}", [N, 2, NG, 2, H, w], F32)
    nn = sb(f"nn{L}", [N, 2, NG, H, w], F32)
    rec = sb(f"rec{L}", [N, 2, R], F32)
    oo = sb(f"oo{L}", [N, 2, NG, D], F32)
    mn = sb(f"mn{L}", [N, 2, NG * D], F32)

    names = ("zeroed ln xt_tr xt e wh erep rmax rdiag max args arg_parts vu ycol y yhi yrest ymid ylo rt rhi rrest rmid rlo masks "
             "s sg pos q t n rec o o_min y_out mn elu y1 dmin dmin_set bn").split()
    s = {n: sem(f"l{L}_{n}") for n in names}
    x_in = [sem(f"l{L}_x_in{r}") for r in range(RING)]
    adj_in = [sem(f"l{L}_adj_in{r}") for r in range(RING)]

    with nc.Block() as block:
        @block.sync
        def _(sp):
            if not first:
                return

            def load(n, slot):
                sp.dma_start(xt[:, slot, :, :], xt_dgn[:, bass.ds(n * NG, NG), :]).then_inc(x_in[slot], 16)
                sp.dma_start(xr[:, slot, :, :], x_ngd[:, bass.ds(n * NG, NG), :]).then_inc(x_in[slot], 16)

            for n in range(RING):
                load(n, n)
            with sp.Fori(1, T // RING) as i:
                for r in range(RING):
                    sp.wait_ge(s["y_out"], (i - 1) * RING + r + 1)
                    load(i * RING + r, r)

        @block.gpsimd
        def _(pool):
            def load_adj(n, slot):
                need(pool, s["masks"], n - RING + 1)
                pool.dma_start(adj[:, slot, :, :], adjt[:, bass.ds(n * NG, NG), :]).then_inc(adj_in[slot], 16)

            def rest(n, slot):
                need(pool, s["yhi"], n + 1)
                need(pool, s["ylo"], n - 1)
                need(pool, s["ymid"], n - 1)
                nc.gpsimd.tensor_tensor(yrest[:, slot % 2, :], yy[:, slot % 2].rearrange("p g k h w -> p (g k h w)"),
                                        yp[0][:, slot].rearrange("p g k h w -> p (g k h w)"),
                                        ALU.subtract).then_inc(s["yrest"], 1)

            def low(n, slot):
                need(pool, s["ymid"], n + 1)
                need(pool, s["q"], 4 * (n - 2))
                nc.gpsimd.tensor_tensor(yp[2][:, slot].rearrange("p g k h w -> p (g k h w)"), yrest[:, slot % 2, :],
                                        yp[1][:, slot].rearrange("p g k h w -> p (g k h w)"),
                                        ALU.subtract).then_inc(s["ylo"], 1)

            def numer(n, slot):
                need(pool, s["t"], 4 * n + 4)
                need(pool, s["o"], n - 1)
                need(pool, s["dmin"], n - 1)
                v = tt[:, slot % 2].rearrange("p g k h w -> p g k (h w)")
                nc.gpsimd.tensor_tensor(nn[:, slot % 2].rearrange("p g h w -> p g (h w)"), v[:, :, 0, :], v[:, :, 1, :],
                                        ALU.add).then_inc(s["n"], 1)

            def finish(n, slot):
                pool.wait_ge(s["zeroed"], 1)
                need(pool, s["o"], n + 1)
                if first:
                    nc.gpsimd.tensor_tensor(yres[:, bass.ds(n * NG, NG), :], oo[:, slot % 2, :, :], xr[:, slot, :, :],
                                            ALU.add).then_inc(s["y_out"], 1)
                else:
                    need(pool, s["y1"], n - 1)
                    nc.gpsimd.tensor_scalar(mn[:, slot % 2, :], oo[:, slot % 2].rearrange("p g d -> p (g d)"), 0.0, None,
                                            ALU.min).then_inc(s["mn"], 1)

            nc.gpsimd.memset(erep[:, :, :, :, :], 0.0).then_inc(s["zeroed"], 1)
            for n in range(2):
                load_adj(n, n)
            rest(0, 0)
            low(0, 0)

            def step(t, slot, lap):
                a0, a1, c0 = (slot + 2) % RING, (slot + 1) % RING, (slot - 1) % RING
                if not known(t) or t + 2 < T:
                    load_adj(t + 2, a0)
                if not known(t) or t >= 1:
                    numer(t - 1, c0)
                if not known(t) or t + 1 < T:
                    rest(t + 1, a1)
                if not known(t) or t >= 1:
                    finish(t - 1, c0)
                if not known(t) or t + 1 < T:
                    low(t + 1, a1)

            steps(pool, step)
            numer(T - 1, (T - 1) % RING)
            finish(T - 1, (T - 1) % RING)

        @block.scalar
        def _(act):
            def evac_xt(n, slot):
                need(act, s["xt_tr"], n + 1)
                need(act, s["wh"], n - 2)
                nc.scalar.copy(xt[:, slot].rearrange("p g n -> p (g n)"), PT[:, :]).then_inc(s["xt"], 1)

            def replicate(n, slot):
                need(act, s["e"], n + 1)
                need(act, s["zeroed"], 1)
                need(act, s["rt"], n - 1)
                need(act, s["args"], n - 1)
                nc.scalar.copy(erep[:, slot % 2, :, :, 0:R],
                               e_ps.rearrange("p k (o r) -> p k o r", o=1).to_broadcast([N, 2, 3, R])).then_inc(s["erep"], 1)

            def exps(n, slot):
                need(act, s["args"], n + 1)
                need(act, s["t"], 4 * (n - 2))
                need(act, s["y"], n - 2)
                nc.scalar.activation(vu[:, slot].rearrange("p k r -> p (k r)"), arg[:, :, :].rearrange("p k r -> p (k r)"),
                                     ACT.Exp).then_inc(s["vu"], 1)

            def row_mid(n, slot):
                need(act, s["rrest"], n + 1)
                nc.scalar.copy(rows[0:64, slot % 2, :, :], rrest[:, :, :]).then_inc(s["rmid"], 1)

            def y_hi(n, slot):
                need(act, s["y"], n + 1)
                need(act, s["q"], 4 * (n - 2))
                nc.scalar.copy(yp[0][:, slot].rearrange("p g k h w -> p (g k h w)"),
                               yy[:, slot % 2].rearrange("p g k h w -> p (g k h w)")).then_inc(s["yhi"], 1)

            def y_mid(n, slot):
                need(act, s["yrest"], n + 1)
                need(act, s["q"], 4 * (n - 2))
                nc.scalar.copy(yp[1][:, slot].rearrange("p g k h w -> p (g k h w)"), yrest[:, slot % 2, :]).then_inc(s["ymid"], 1)

            def sign(n, u, z):
                m = n * U + u
                need(act, s["s"], m + 1)
                need(act, s["pos"], m - 1)
                nc.scalar.activation(sg[:, z, :], S[z][:, :], ACT.Sign).then_inc(s["sg"], 1)

            def elu(n, slot):
                need(act, s["mn"], n + 1)
                nc.scalar.activation(mn[:, slot % 2, :], mn[:, slot % 2, :], ACT.Exp).then_inc(s["elu"], 1)

            def zslot(slot, u):
                return u % 2 if U > 1 else slot % 2

            if not first:
                evac_xt(0, 0)
            replicate(0, 0)
            if not first:
                evac_xt(1, 1)
            replicate(1, 1)
            exps(0, 0)
            row_mid(0, 0)
            y_hi(0, 0)
            y_mid(0, 0)
            sign(0, 0, 0)

            def step(t, slot, lap):
                a0, a1, c0 = (slot + 2) % RING, (slot + 1) % RING, (slot - 1) % RING
                in0 = not known(t) or t + 2 < T
                in1 = not known(t) or t + 1 < T
                inc = not known(t) or t >= 1
                if in1:
                    exps(t + 1, a1)
                if U > 1:
                    sign(t, 1, zslot(slot, 1))
                if in1:
                    row_mid(t + 1, a1)
                    if not first and in0:
                        evac_xt(t + 2, a0)
                    y_hi(t + 1, a1)
                if U > 1:
                    sign(t, 2, zslot(slot, 2))
                if in0:
                    replicate(t + 2, a0)
                if U > 1:
                    sign(t, 3, zslot(slot, 3))
                if not first and inc:
                    elu(t - 1, c0)
                if in1:
                    y_mid(t + 1, a1)
                    sign(t + 1, 0, zslot(slot + 1, 0))

            steps(act, step)
            if not first:
                elu(T - 1, (T - 1) % RING)

        @block.vector
        def _(dve):
            def normalize(n, slot):
                need(dve, s["y_out"], n - 3)
                need(dve, s["xt_tr"], n - 3)
                for g in range(NG):
                    at = n * NG + g
                    ins = nc.vector.tensor_scalar(xr[:, slot, g, :], yres[:, bass.ds(at, 1), :].rearrange("p o d -> p (o d)"),
                                                  mean[:, bass.ds(at, 1)], rstd[:, bass.ds(at, 1)], ALU.subtract, ALU.mult)
                ins.then_inc(s["ln"], 1)

            def args(n, slot):
                e1, e2 = erep[:, slot % 2, 0, 0, 0:R], erep[:, slot % 2, 1, 0, 0:R]
                need(dve, s["max"], n + 1)
                need(dve, s["vu"], n)
                nc.vector.tensor_tensor(arg[:, 0, :], e2, m_ps, ALU.subtract)
                nc.vector.tensor_tensor(cc[:, :], e1, m_ps, ALU.add).then_inc(s["arg_parts"], 1)
                need(dve, s["arg_parts"], n + 1)
                nc.vector.tensor_scalar(arg[:, 1, :], arg[:, 0, :], 0.2, None, ALU.mult)
                nc.vector.tensor_scalar(arg[:, 2, :], cc[:, :], 0.8, 0.0, ALU.mult, ALU.min)
                nc.vector.tensor_scalar(arg[:, 3, :], cc[:, :], -0.8, 0.0, ALU.mult, ALU.min).then_inc(s["args"], 1)

            def masks(n, slot, lap):
                need(dve, adj_in[slot], 16 * (lap + 1))
                need(dve, s["q"], 4 * (n - 2))
                nc.vector.tensor_scalar(nota[:, slot], adj[:, slot], -1.0, 1.0, ALU.mult, ALU.add)
                nc.vector.tensor_scalar(nega[:, slot], adj[:, slot], -1.0, None, ALU.mult).then_inc(s["masks"], 1)

            def row_max(n, slot):
                need(dve, s["rt"], n + 1)
                need(dve, s["rdiag"], n)
                nc.vector.reduce_max(rmax[:, :], t_ps[0:32, 1, :], AX_X).then_inc(s["rmax"], 1)
                need(dve, s["rmax"], n + 1)
                need(dve, s["max"], n)
                nc.vector.tensor_scalar(rdiag[:, :], k["ident"][0:32, 0:R], rmax[:, 0:1], None, ALU.mult).then_inc(s["rdiag"], 1)

            def row_hi(n, slot):
                need(dve, s["s"], U * (n - 1))
                nc.vector.tensor_copy(rows[:, slot % 2, :, :], t_ps).then_inc(s["rhi"], 1)

            def row_rest(n, slot):
                need(dve, s["rhi"], n + 1)
                need(dve, s["rlo"], n)
                need(dve, s["rmid"], n)
                nc.vector.tensor_tensor(rrest[:, :, :], t_ps[0:64], rows[0:64, slot % 2, :, :], ALU.subtract).then_inc(s["rrest"], 1)

            def row_low(n, slot):
                need(dve, s["rmid"], n + 1)
                nc.vector.tensor_tensor(rows[0:32, slot % 2, :, :], rrest[0:32, :, :], rows[0:32, slot % 2, :, :],
                                        ALU.subtract).then_inc(s["rlo"], 1)

            def y_columns(n, slot):
                need(dve, s["vu"], n + 1)
                need(dve, s["yrest"], n - 1)
                for kind, f in ((0, 1.0), (1, -1.0)):
                    ins = nc.vector.tensor_scalar(yy[:, slot % 2, :, kind, :, hd],
                                                  vu[:, slot, kind, :].rearrange("p (g h) -> p g h", g=NG), f, None, ALU.mult)
                ins.then_inc(s["ycol"], 1)

            def y_products(n, slot, graphs):
                if graphs[0] == 0:
                    need(dve, s["wh"], n + 1)
                    need(dve, s["ycol"], n + 1)
                for g in graphs:
                    wh = W[:, g * D:(g + 1) * D].rearrange("p (o h d) -> p o h d", o=1, d=hd).to_broadcast([N, 2, H, hd])
                    ins = nc.vector.tensor_tensor(yy[:, slot % 2, g, :, :, 0:hd], wh,
                                                  yy[:, slot % 2, g, :, :, hd:w].to_broadcast([N, 2, H, hd]), ALU.mult)
                if graphs[-1] == NG - 1:
                    ins.then_inc(s["y"], 1)

            def positive(n, u, slot, z):
                m = n * U + u
                need(dve, s["sg"], m + 1)
                need(dve, s["q"], gpu * (m - 1))
                if u == 0:
                    need(dve, s["masks"], n + 1)
                if first:
                    shape = [N, H, N]
                    nc.vector.tensor_tensor(pos[:, z, :].rearrange("p (h n) -> p h n", h=H), sg[:, z, :].rearrange("p (h n) -> p h n", h=H),
                                            nota[:, slot, u:u + 1, :].to_broadcast(shape), ALU.is_gt).then_inc(s["pos"], 1)
                else:
                    nc.vector.tensor_tensor(pos[:, z, :], sg[:, z, :], nota[:, slot].rearrange("p g n -> p (g n)"),
                                            ALU.is_gt).then_inc(s["pos"], 1)

            def weigh(n, g, slot):
                need(dve, s["q"], 4 * n + g + 1)
                need(dve, s["n"], n - 1)
                q = Q[g % 2][:, 0:2 * kin].rearrange("p (k h w) -> p k h w", k=2, w=w)
                u = vu[:, slot, 2:4, g * H:(g + 1) * H].rearrange("p k (h o) -> p k h o", o=1).to_broadcast([N, 2, H, w])
                nc.vector.tensor_tensor(tt[:, slot % 2, g], q, u, ALU.mult).then_inc(s["t"], 1)

            def divide(n, slot):
                need(dve, s["n"], n + 1)
                need(dve, s["y_out"], n - 1)
                need(dve, s["mn"], n - 1) if not first else None
                den = nn[:, slot % 2, :, :, hd:w].rearrange("p g h o -> p (g h o)")
                nc.vector.reciprocal(rec[:, slot % 2, :], den).then_inc(s["rec"], 1)
                need(dve, s["dmin"], n)
                nc.vector.tensor_tensor(dmin[:, 0:R], dmin[:, 0:R], den, ALU.min).then_inc(s["dmin"], 1)
                need(dve, s["rec"], n + 1)
                nc.vector.tensor_tensor(oo[:, slot % 2].rearrange("p g (h d) -> p (g h) d", h=H),
                                        nn[:, slot % 2, :, :, 0:hd].rearrange("p g h d -> p (g h) d"),
                                        rec[:, slot % 2, :].rearrange("p (r o) -> p r o", o=1).to_broadcast([N, R, hd]),
                                        ALU.mult).then_inc(s["o"], 1)

            def finish(n, slot):
                if not first:
                    o = oo[:, slot % 2].rearrange("p g d -> p (g d)")
                    m = mn[:, slot % 2, :]
                    need(dve, s["elu"], n + 1)
                    nc.vector.scalar_tensor_tensor(o, o, 0.0, m, ALU.max, ALU.add).then_inc(s["y1"], 1)
                    need(dve, s["y1"], n + 1)
                    nc.vector.scalar_tensor_tensor(yres[:, bass.ds(n * NG, NG), :], oo[:, slot % 2, :, :], -1.0,
                                                   xr[:, slot, :, :], ALU.add, ALU.add).then_inc(s["y_out"], 1)

            def statistics(n, slot):
                need(dve, s["y_out"], n + 1)
                for g in range(NG):
                    at = n * NG + g
                    nc.vector.bn_stats(stats[:, bass.ds(at, 1), :].rearrange("p o d -> p (o d)"),
                                       yres[:, bass.ds(at, 1), :].rearrange("p o d -> p (o d)"))

            def zslot(slot, u):
                return u % 2 if U > 1 else slot % 2

            if first:
                nc.vector.memset(dmin[:, :], 1.0).then_inc(s["dmin_set"], 1)
                dve.wait_ge(s["dmin_set"], 1)
            if not first:
                normalize(0, 0)
                normalize(1, 1)
            row_max(0, 0)
            args(0, 0)
            masks(0, 0, 0)
            row_hi(0, 0)
            row_rest(0, 0)
            row_low(0, 0)
            row_max(1, 1)
            y_columns(0, 0)
            y_products(0, 0, range(NG))

            def step(t, slot, lap):
                a0, a1, c0 = (slot + 2) % RING, (slot + 1) % RING, (slot - 1) % RING
                in0 = not known(t) or t + 2 < T
                in1 = not known(t) or t + 1 < T
                inc = not known(t) or t >= 1
                if not first and in0:
                    normalize(t + 2, a0)
                positive(t, 0, slot, zslot(slot, 0))
                if in1:
                    args(t + 1, a1)
                    row_hi(t + 1, a1)
                    masks(t + 1, a1, lap + (slot + 1) // RING)
                    row_rest(t + 1, a1)
                if U > 1:
                    positive(t, 1, slot, zslot(slot, 1))
                weigh(t, 0, slot)
                if in1:
                    row_low(t + 1, a1)
                    y_columns(t + 1, a1)
                    y_products(t + 1, a1, range(2))
                if not first:
                    weigh(t, 1, slot)
                if in1:
                    y_products(t + 1, a1, range(2, NG))
                if U > 1:
                    positive(t, 2, slot, zslot(slot, 2))
                if first:
                    weigh(t, 1, slot)
                if inc:
                    divide(t - 1, c0)
                if U > 1:
                    positive(t, 3, slot, zslot(slot, 3))
                weigh(t, 2, slot)
                if inc:
                    finish(t - 1, c0)
                    statistics(t - 1, c0)
                if in0:
                    row_max(t + 2, a0)
                weigh(t, 3, slot)

            steps(dve, step)
            divide(T - 1, (T - 1) % RING)
            finish(T - 1, (T - 1) % RING)
            statistics(T - 1, (T - 1) % RING)

        @block.tensor
        def _(pe):
            def transpose_x(n, slot):
                need(pe, s["ln"], n + 1)
                need(pe, s["xt"], n)
                for g in range(NG):
                    ins = nc.tensor.transpose(PT[:, g * N:(g + 1) * N], xr[:, slot, g, :], k["ident"][:, :])
                ins.then_inc(s["xt_tr"], 1)

            def e_columns(n, slot, lap):
                if first:
                    need(pe, x_in[slot], 32 * (lap + 1))
                else:
                    need(pe, s["xt"], n + 1)
                need(pe, s["erep"], n)
                need(pe, s["rrest"], n)
                need(pe, s["args"], n)
                for g in range(NG):
                    ins = nc.tensor.matmul(e_ps[:, :, g * H:(g + 1) * H], xt[:, slot, g, :],
                                           wa[:, :].rearrange("d (k h) -> d k h", k=2), start=True, stop=True)
                ins.then_inc(s["e"], 1)

            def wh(n, slot):
                need(pe, s["y"], n)
                for g in range(NG):
                    ins = nc.tensor.matmul(W[:, g * D:(g + 1) * D], xt[:, slot, g, :], wm[:, :], start=True, stop=True)
                ins.then_inc(s["wh"], 1)

            def e_rows(n, slot):
                need(pe, s["erep"], n + 1)
                need(pe, s["rrest"], n)
                for e in range(2):
                    ins = nc.tensor.transpose(t_ps[:, e, :], erep[:, slot % 2, e, :, :].rearrange("p a r -> p (a r)"), k["ident"][:, :])
                ins.then_inc(s["rt"], 1)

            def maxima(n, slot):
                need(pe, s["rdiag"], n + 1)
                nc.tensor.matmul(m_ps, k["onesf"][:, :], rdiag[:, :], start=True, stop=True).then_inc(s["max"], 1)

            def scores(n, u, slot, z):
                m = n * U + u
                if u == 0:
                    need(pe, s["rlo"], n + 1)
                need(pe, s["sg"], m - 1)
                r1, r2 = rows[:, slot % 2, 0, :], rows[:, slot % 2, 1, :]
                for half in range(2 if first else 1):
                    at = u * H + half * 4
                    nc.tensor.matmul(S[z][:, half * BANK:(half + 1) * BANK], r2,
                                     k["sel"][:, at:at + 4, :].rearrange("p r n -> p (r n)"),
                                     start=True, stop=False, skip_group_check=True)
                    for q in range(4):
                        ins = nc.tensor.matmul(S[z][:, half * BANK + q * N:half * BANK + (q + 1) * N], k["sel"][:, at + q, :], r1,
                                               start=False, stop=(q == 3), skip_group_check=True)
                ins.then_inc(s["s"], 1)

            def attend(n, g, slot, z):
                q = Q[g % 2]
                qk = q[:, 0:2 * kin].rearrange("p (k h w) -> p k h w", k=2, w=w)
                if g % gpu == 0:
                    need(pe, s["pos"], n * U + g // gpu + 1)
                need(pe, s["t"], 4 * n + g - 1)
                if g == 0:
                    need(pe, s["ylo"], n + 1)
                for p in range(3):
                    nc.tensor.matmul(q[:, kin:2 * kin], nega[:, slot, g, :], yp[p][:, slot, g, 1].rearrange("p h w -> p (h w)"),
                                     start=(p == 0), stop=False, skip_group_check=True)
                for h in range(H):
                    at = (h if first else g) * N
                    for p in range(3):
                        last = h == H - 1 and p == 2
                        ins = nc.tensor.matmul(qk[:, :, h, :], pos[:, z, at:at + N], yp[p][:, slot, g, :, h, :],
                                               start=False, stop=last, skip_group_check=True)
                ins.then_inc(s["q"], 1)

            def zslot(slot, u):
                return u % 2 if U > 1 else slot % 2

            if not first:
                transpose_x(0, 0)
            e_columns(0, 0, 0)
            wh(0, 0)
            if not first:
                transpose_x(1, 1)
            e_rows(0, 0)
            maxima(0, 0)
            e_columns(1, 1, 0)
            e_rows(1, 1)
            maxima(1, 1)
            scores(0, 0, 0, 0)
            wh(1, 1)

            def step(t, slot, lap):
                a0, a1 = (slot + 2) % RING, (slot + 1) % RING
                in0 = not known(t) or t + 2 < T
                in1 = not known(t) or t + 1 < T
                lap0 = lap + (slot + 2) // RING
                if first:
                    scores(t, 1, slot, zslot(slot, 1))
                attend(t, 0, slot, zslot(slot, 0))
                if first:
                    scores(t, 2, slot, zslot(slot, 2))
                attend(t, 1, slot, zslot(slot, 1) if first else zslot(slot, 0))
                if in0:
                    if not first:
                        transpose_x(t + 2, a0)
                    else:
                        e_columns(t + 2, a0, lap0)
                if first:
                    scores(t, 3, slot, zslot(slot, 3))
                attend(t, 2, slot, zslot(slot, 2) if first else zslot(slot, 0))
                if in0 and first:
                    e_rows(t + 2, a0)
                    wh(t + 2, a0)
                if in1 and first:
                    scores(t + 1, 0, a1, zslot(slot + 1, 0))
                if in0 and first:
                    maxima(t + 2, a0)
                attend(t, 3, slot, zslot(slot, 3) if first else zslot(slot, 0))
                if not first:
                    if in0:
                        e_columns(t + 2, a0, lap0)
                    if in1:
                        scores(t + 1, 0, a1, zslot(slot + 1, 0))
                    if in0:
                        e_rows(t + 2, a0)
                        wh(t + 2, a0)
                        maxima(t + 2, a0)

            steps(pe, step)


def row_statistics(nc, sb, sem, L, stats, mean, rstd):
    s = {n: sem(f"st{L}_{n}") for n in ("var", "root", "link")}
    d = sb(f"sd{L}", [N, B], F32)
    v = sb(f"sv{L}", [N, B], F32)
    me, ve, mo, vo = (stats[:, :, n] for n in (1, 2, 4, 5))
    with nc.Block() as block:
        @block.vector
        def _(dve):
            nc.vector.tensor_tensor(mean[:, :], me, mo, ALU.add).then_inc(s["link"], 1)
            nc.vector.tensor_tensor(d[:, :], me, mo, ALU.subtract).then_inc(s["link"], 1)
            nc.vector.tensor_tensor(v[:, :], ve, vo, ALU.add).then_inc(s["link"], 1)
            dve.wait_ge(s["link"], 3)
            nc.vector.tensor_scalar(mean[:, :], mean[:, :], 0.5, None, ALU.mult)
            nc.vector.scalar_tensor_tensor(d[:, :], d[:, :], 0.25, d[:, :], ALU.mult, ALU.mult).then_inc(s["link"], 1)
            nc.vector.tensor_scalar(v[:, :], v[:, :], 1.0 / D, EPS, ALU.mult, ALU.add).then_inc(s["link"], 1)
            dve.wait_ge(s["link"], 5)
            nc.vector.tensor_tensor(v[:, :], v[:, :], d[:, :], ALU.add).then_inc(s["var"], 1)
            dve.wait_ge(s["root"], 1)
            nc.vector.reciprocal(rstd[:, :], v[:, :])

        @block.scalar
        def _(act):
            act.wait_ge(s["var"], 1)
            nc.scalar.activation(v[:, :], v[:, :], ACT.Sqrt).then_inc(s["root"], 1)


def normalized(nc, dve, s, xr, yres, mean, rstd, n, slot):
    for g in range(NG):
        at = n * NG + g
        ins = nc.vector.tensor_scalar(xr[:, slot, g, :], yres[:, bass.ds(at, 1), :].rearrange("p o d -> p (o d)"),
                                      mean[:, bass.ds(at, 1)], rstd[:, bass.ds(at, 1)], ALU.subtract, ALU.mult)
    ins.then_inc(s["ln"], 1)


def relational(nc, sb, sem, pb, k, yres, stats, mean, rstd, adjbad, adj_mgn):
    PT, HG, O = pb[0], [pb.pair(1), pb.pair(3)], [pb[5], pb[6]]
    xr = sb("x2", [N, RING, NG, D], F32)
    xt = sb("xt2", [D, 2, NG, N], F32)
    adj = sb("adj2", [N, RING, NG, N], BF16)
    th = sb("th2", [N, 2, NG, D], F32)
    vv = sb("vv2", [N, 2, NG, D], F32)
    vrest = sb("vrest2", [N, 2, NG, D], F32)
    vp = [sb(f"v{p}2", [N, 2, NG, D], BF16) for p in ("hi", "mid", "lo")]
    sq = sb("sq2", [N, NG * N], BF16)
    s = {n: sem(f"l2_{n}") for n in "ln xt_tr xt hg tanh v vhi vrest vmid vlo o y_out y1 check".split()}
    adj_in = [sem(f"l2_adj_in{r}") for r in range(RING)]
    y1 = sb("y12", [N, NG, D], F32)

    with nc.Block() as block:
        @block.gpsimd
        def _(pool):
            def load_adj(n, slot):
                need(pool, s["o"], n - 3)
                need(pool, s["check"], n - 3)
                pool.dma_start(adj[:, slot, :, :], adj_mgn[:, bass.ds(n * NG, NG), :]).then_inc(adj_in[slot], 16)

            def rest(n, slot):
                need(pool, s["vhi"], n + 1)
                need(pool, s["vmid"], n - 1)
                need(pool, s["vlo"], n - 1)
                nc.gpsimd.tensor_tensor(vrest[:, slot % 2], vv[:, slot % 2], vp[0][:, slot % 2], ALU.subtract).then_inc(s["vrest"], 1)

            def low(n, slot):
                need(pool, s["vmid"], n + 1)
                need(pool, s["o"], n - 1)
                nc.gpsimd.tensor_tensor(vp[2][:, slot % 2], vrest[:, slot % 2], vp[1][:, slot % 2], ALU.subtract).then_inc(s["vlo"], 1)

            load_adj(0, 0)
            load_adj(1, 1)
            rest(0, 0)
            low(0, 0)

            def step(t, slot, lap):
                if not known(t) or t + 2 < T:
                    load_adj(t + 2, (slot + 2) % RING)
                if not known(t) or t + 1 < T:
                    rest(t + 1, (slot + 1) % RING)
                    low(t + 1, (slot + 1) % RING)

            steps(pool, step)

        @block.scalar
        def _(act):
            def evac_xt(n, slot):
                need(act, s["xt_tr"], n + 1)
                need(act, s["hg"], n - 1)
                nc.scalar.copy(xt[:, slot % 2].rearrange("p g n -> p (g n)"), PT[:, :]).then_inc(s["xt"], 1)

            def tanh(n, slot):
                need(act, s["hg"], n + 1)
                need(act, s["v"], n - 1)
                g = HG[slot % 2].rearrange("p (g k d) -> p g k d", g=NG, k=2)[:, :, 1, :]
                nc.scalar.activation(th[:, slot % 2], g, ACT.Tanh, scale=0.5).then_inc(s["tanh"], 1)

            def high(n, slot):
                need(act, s["v"], n + 1)
                need(act, s["o"], n - 1)
                nc.scalar.copy(vp[0][:, slot % 2], vv[:, slot % 2]).then_inc(s["vhi"], 1)

            def mid(n, slot):
                need(act, s["vrest"], n + 1)
                nc.scalar.copy(vp[1][:, slot % 2], vrest[:, slot % 2]).then_inc(s["vmid"], 1)

            def check(n, slot, lap):
                need(act, adj_in[slot], 16 * (lap + 1))
                need(act, s["check"], n)
                nc.scalar.activation(sq[:, :], adj[:, slot].rearrange("p g n -> p (g n)"), ACT.Square, bias=k["minushalf"][:, :],
                                     accum_out=adjbad[:, bass.ds(n, 1)]).then_inc(s["check"], 1)

            evac_xt(0, 0)
            tanh(0, 0)
            evac_xt(1, 1)
            high(0, 0)
            mid(0, 0)

            def step(t, slot, lap):
                a0, a1 = (slot + 2) % RING, (slot + 1) % RING
                if not known(t) or t + 1 < T:
                    tanh(t + 1, a1)
                check(t, slot, lap)
                if not known(t) or t + 1 < T:
                    high(t + 1, a1)
                if not known(t) or t + 2 < T:
                    evac_xt(t + 2, a0)
                if not known(t) or t + 1 < T:
                    mid(t + 1, a1)

            steps(act, step)

        @block.vector
        def _(dve):
            def normalize(n, slot):
                need(dve, s["y_out"], n - 3)
                need(dve, s["xt_tr"], n - 3)
                normalized(nc, dve, s, xr, yres, mean, rstd, n, slot)

            def values(n, slot):
                need(dve, s["tanh"], n + 1)
                need(dve, s["vrest"], n - 1)
                h = HG[slot % 2].rearrange("p (g k d) -> p g k d", g=NG, k=2)[:, :, 0, :]
                nc.vector.scalar_tensor_tensor(vv[:, slot % 2], th[:, slot % 2], 1.0, h, ALU.add, ALU.mult).then_inc(s["v"], 1)

            def finish(n, slot):
                need(dve, s["o"], n + 1)
                nc.vector.scalar_tensor_tensor(yres[:, bass.ds(n * NG, NG), :], O[slot % 2].rearrange("p (g d) -> p g d", g=NG), 0.0,
                                               xr[:, slot, :, :], ALU.max, ALU.add).then_inc(s["y_out"], 1)

            def statistics(n, slot):
                need(dve, s["y_out"], n + 1)
                for g in range(NG):
                    at = n * NG + g
                    nc.vector.bn_stats(stats[:, bass.ds(at, 1), :].rearrange("p o d -> p (o d)"),
                                       yres[:, bass.ds(at, 1), :].rearrange("p o d -> p (o d)"))

            normalize(0, 0)
            normalize(1, 1)
            values(0, 0)

            def step(t, slot, lap):
                if not known(t) or t + 2 < T:
                    normalize(t + 2, (slot + 2) % RING)
                if not known(t) or t >= 1:
                    finish(t - 1, (slot - 1) % RING)
                if not known(t) or t + 1 < T:
                    values(t + 1, (slot + 1) % RING)
                if not known(t) or t >= 1:
                    statistics(t - 1, (slot - 1) % RING)

            steps(dve, step)
            finish(T - 1, (T - 1) % RING)
            statistics(T - 1, (T - 1) % RING)

        @block.tensor
        def _(pe):
            def transpose_x(n, slot):
                need(pe, s["ln"], n + 1)
                need(pe, s["xt"], n)
                for g in range(NG):
                    ins = nc.tensor.transpose(PT[:, g * N:(g + 1) * N], xr[:, slot, g, :], k["ident"][:, :])
                ins.then_inc(s["xt_tr"], 1)

            def hidden(n, slot):
                need(pe, s["xt"], n + 1)
                need(pe, s["v"], n - 1)
                for g in range(NG):
                    out = HG[slot % 2][:, g * 2 * D:(g + 1) * 2 * D]
                    nc.tensor.matmul(out, k["ones96"][:, :], k["bias2"][:, :], start=True, stop=False, skip_group_check=True)
                    ins = nc.tensor.matmul(out, xt[:, slot % 2, g, :], k["w2"][:, :], start=False, stop=True, skip_group_check=True)
                ins.then_inc(s["hg"], 1)

            def gather(n, slot, lap):
                need(pe, adj_in[slot], 16 * (lap + 1))
                need(pe, s["vlo"], n + 1)
                need(pe, s["y_out"], n - 1)
                for g in range(NG):
                    for p in range(3):
                        ins = nc.tensor.matmul(O[slot % 2][:, g * D:(g + 1) * D], adj[:, slot, g, :], vp[p][:, slot % 2, g, :],
                                               start=(p == 0), stop=(p == 2), skip_group_check=True)
                ins.then_inc(s["o"], 1)

            transpose_x(0, 0)
            hidden(0, 0)
            transpose_x(1, 1)

            def step(t, slot, lap):
                if not known(t) or t + 1 < T:
                    hidden(t + 1, (slot + 1) % RING)
                if not known(t) or t + 2 < T:
                    transpose_x(t + 2, (slot + 2) % RING)
                gather(t, slot, lap)

            steps(pe, step)


def heads(nc, sb, sem, pb, k, yres, stats, mean, rstd, dmin, adjt):
    H, E = 4, 32
    w = E + 1
    SCALE = E ** -0.5
    S = [pb[h] for h in range(H)]
    PT, QV, O, KF = pb[4], pb[5], pb[6], pb[7]
    f_row, f_all = O[0:1, 384:384 + N], O[:, 380:381]
    xr = sb("x3", [N, RING, NG, D], F32)
    xt = sb("xt3", [D, 2, NG * N], F32)
    adj = sb("adj3", [N, RING, NG * N], BF16)
    qt = sb("qt3", [D, 2, NG * N], F32)
    kt = sb("kt3", [D, 2, NG * N], F32)
    q2 = sb("q23", [D, 2, NG * N], BF16)
    k2 = sb("k23", [D, 2, NG * N], BF16)
    va = sb("va3", [N, 2, NG, H, w], F32)
    pp = sb("pp3", [N, 2, H, NG * N], F32)
    fm = sb("fm3", [N, 2], F32)
    f1 = sb("f13", [1, 2], F32)
    nb = sb("nb3", [N, 2], F32)
    rec = sb("rec3", [N, 2, 2, H], F32)
    on = sb("on3", [N, 2, NG, D], F32)
    ont = sb("ont3", [D, NG * N], F32)
    s = {n: sem(f"l3_{n}") for n in ("zeroed ln xt_tr xt q qt kk kt v va q2 k2 f fm frow f1 fall nb s p pm pmp o rec dmin on ont_tr ont "
                                     "w y_out").split()}
    adj_in = [sem(f"l3_adj_in{r}") for r in range(RING)]
    POOLED = 1

    with nc.Block() as block:
        @block.gpsimd
        def _(pool):
            def load_adj(n, slot):
                need(pool, s["pm"], (H - POOLED) * (n - 3))
                pool.dma_start(adj[:, slot, :].rearrange("p (g n) -> p g n", g=NG),
                               adjt[:, bass.ds(n * NG, NG), :]).then_inc(adj_in[slot], 16)

            def squares(n, slot):
                for a, b, ready, done in ((qt, q2, "qt", "q2"), (kt, k2, "kt", "k2")):
                    need(pool, s[ready], n + 1)
                    need(pool, s["f"], n - 1)
                    nc.gpsimd.tensor_tensor(b[:, slot % 2], a[:, slot % 2], a[:, slot % 2], ALU.mult).then_inc(s[done], 1)

            def mask(n, slot, lap):
                for h in range(H - POOLED, H):
                    need(pool, s["p"], H * n + h + 1)
                    need(pool, adj_in[slot], 16 * (lap + 1))
                    nc.gpsimd.tensor_tensor(pp[:, slot % 2, h], pp[:, slot % 2, h], adj[:, slot], ALU.mult).then_inc(s["pmp"], 1)

            load_adj(0, 0)
            load_adj(1, 1)
            squares(0, 0)

            def step(t, slot, lap):
                if not known(t) or t + 2 < T:
                    load_adj(t + 2, (slot + 2) % RING)
                if not known(t) or t + 1 < T:
                    squares(t + 1, (slot + 1) % RING)
                mask(t, slot, lap)

            steps(pool, step)

        @block.scalar
        def _(act):
            def evac_xt(n, slot):
                need(act, s["xt_tr"], n + 1)
                need(act, s["v"], n - 1)
                nc.scalar.copy(xt[:, slot % 2, :], PT[:, :]).then_inc(s["xt"], 1)

            def evac_q(n, slot):
                need(act, s["q"], n + 1)
                need(act, s["s"], H * (n - 1))
                need(act, s["q2"], n - 1)
                nc.scalar.copy(qt[:, slot % 2, :], QV[:, :]).then_inc(s["qt"], 1)

            def exps(n, h, slot):
                need(act, s["s"], H * n + h + 1)
                if h == 0:
                    need(act, s["nb"], n + 1)
                    need(act, s["o"], 2 * (n - 1))
                nc.scalar.activation(pp[:, slot % 2, h], S[h][:, :], ACT.Exp, bias=nb[:, slot % 2:slot % 2 + 1],
                                     scale=SCALE).then_inc(s["p"], 1)

            def evac_on(n, slot):
                need(act, s["ont_tr"], n + 1)
                need(act, s["w"], n)
                nc.scalar.copy(ont[:, :], PT[:, :]).then_inc(s["ont"], 1)

            evac_xt(0, 0)
            evac_q(0, 0)
            evac_xt(1, 1)

            def step(t, slot, lap):
                exps(t, 0, slot)
                exps(t, 1, slot)
                if not known(t) or t + 1 < T:
                    evac_q(t + 1, (slot + 1) % RING)
                exps(t, 2, slot)
                if not known(t) or t >= 1:
                    evac_on(t - 1, (slot - 1) % RING)
                exps(t, 3, slot)
                if not known(t) or t + 2 < T:
                    evac_xt(t + 2, (slot + 2) % RING)

            steps(act, step)
            evac_on(T - 1, (T - 1) % RING)

        @block.vector
        def _(dve):
            def normalize(n, slot):
                need(dve, s["y_out"], n - 3)
                need(dve, s["xt_tr"], n - 3)
                normalized(nc, dve, s, xr, yres, mean, rstd, n, slot)

            def evac_k(n, slot):
                need(dve, s["kk"], n + 1)
                need(dve, s["s"], H * (n - 1))
                need(dve, s["k2"], n - 1)
                nc.vector.tensor_copy(kt[:, slot % 2, :], KF[:, :]).then_inc(s["kt"], 1)

            def evac_v(n, slot):
                need(dve, s["v"], n + 1)
                need(dve, s["o"], 2 * (n - 1))
                nc.vector.tensor_copy(va[:, slot % 2, :, :, 0:E].rearrange("p g h e -> p (g h) e"),
                                      QV[:, :].rearrange("p (r e) -> p r e", e=E)).then_inc(s["va"], 1)

            def bound(n, slot):
                need(dve, s["f"], n + 1)
                need(dve, s["frow"], n - 1)
                nc.vector.reduce_max(fm[:, slot % 2:slot % 2 + 1], KF[:, :], AX_X).then_inc(s["fm"], 1)

            def negate(n, slot):
                need(dve, s["frow"], n + 1)
                nc.vector.reduce_max(f1[0:1, slot % 2:slot % 2 + 1], f_row, AX_X).then_inc(s["f1"], 1)
                need(dve, s["fall"], n + 1)
                need(dve, s["p"], H * (n - 1))
                nc.vector.tensor_scalar(nb[:, slot % 2:slot % 2 + 1], f_all, -SCALE, None, ALU.mult).then_inc(s["nb"], 1)

            def mask(n, h, slot, lap):
                need(dve, s["p"], H * n + h + 1)
                need(dve, adj_in[slot], 16 * (lap + 1))
                nc.vector.tensor_tensor(pp[:, slot % 2, h], pp[:, slot % 2, h], adj[:, slot], ALU.mult).then_inc(s["pm"], 1)

            def divide(n, pair, slot):
                need(dve, s["o"], 2 * n + pair + 1)
                need(dve, s["ont_tr"], n - 1)
                need(dve, s["on"], 2 * n + pair - 1)
                o = O[:, 0:2 * H * w].rearrange("p (g h w) -> p g h w", g=2, h=H)
                den = O[:, 0:2 * H * w].rearrange("p (r w) -> p r w", w=w)[:, :, E]
                m = 2 * n + pair
                nc.vector.reciprocal(rec[:, pair].rearrange("p g h -> p (g h)"), den).then_inc(s["rec"], 1)
                need(dve, s["dmin"], m)
                nc.vector.tensor_tensor(dmin[:, 0:2 * H], dmin[:, 0:2 * H], den, ALU.min).then_inc(s["dmin"], 1)
                need(dve, s["rec"], m + 1)
                nc.vector.tensor_tensor(on[:, slot % 2, 2 * pair:2 * pair + 2].rearrange("p g (h e) -> p (g h) e", h=H),
                                        O[:, 0:2 * H * w].rearrange("p (r w) -> p r w", w=w)[:, :, 0:E],
                                        rec[:, pair].rearrange("p g (h o) -> p (g h) o", o=1).to_broadcast([N, 2 * H, E]),
                                        ALU.mult).then_inc(s["on"], 1)

            def finish(n, slot):
                need(dve, s["w"], n + 1)
                nc.vector.tensor_tensor(yres[:, bass.ds(n * NG, NG), :], KF[:, :].rearrange("p (g d) -> p g d", g=NG),
                                        xr[:, slot, :, :], ALU.add).then_inc(s["y_out"], 1)

            def statistics(n, slot):
                need(dve, s["y_out"], n + 1)
                for g in range(NG):
                    at = n * NG + g
                    nc.vector.bn_stats(stats[:, bass.ds(at, 1), :].rearrange("p o d -> p (o d)"),
                                       yres[:, bass.ds(at, 1), :].rearrange("p o d -> p (o d)"))

            nc.vector.memset(va[:, :, :, :, :], 1.0).then_inc(s["zeroed"], 1)
            dve.wait_ge(s["zeroed"], 1)
            normalize(0, 0)
            normalize(1, 1)
            evac_k(0, 0)
            evac_v(0, 0)
            bound(0, 0)

            def step(t, slot, lap):
                a0, a1, c0 = (slot + 2) % RING, (slot + 1) % RING, (slot - 1) % RING
                in0 = not known(t) or t + 2 < T
                in1 = not known(t) or t + 1 < T
                inc = not known(t) or t >= 1
                negate(t, slot)
                if in0:
                    normalize(t + 2, a0)
                mask(t, 0, slot, lap)
                mask(t, 1, slot, lap)
                if in1:
                    evac_k(t + 1, a1)
                mask(t, 2, slot, lap)
                if in1:
                    evac_v(t + 1, a1)
                if inc:
                    finish(t - 1, c0)
                    statistics(t - 1, c0)
                divide(t, 0, slot)
                if in1:
                    bound(t + 1, a1)
                divide(t, 1, slot)

            steps(dve, step)
            finish(T - 1, (T - 1) % RING)
            statistics(T - 1, (T - 1) % RING)

        @block.tensor
        def _(pe):
            def transpose_x(n, slot):
                need(pe, s["ln"], n + 1)
                need(pe, s["xt"], n)
                need(pe, s["ont"], n - 2)
                for g in range(NG):
                    ins = nc.tensor.transpose(PT[:, g * N:(g + 1) * N], xr[:, slot, g, :], k["ident"][:, :])
                ins.then_inc(s["xt_tr"], 1)

            def queries(n, slot):
                need(pe, s["xt"], n + 1)
                need(pe, s["va"], n)
                nc.tensor.matmul(QV[:, :], k["w3q"][:, :], xt[:, slot % 2, :], start=True, stop=True).then_inc(s["q"], 1)

            def keys(n, slot):
                need(pe, s["fm"], n)
                need(pe, s["y_out"], n - 2)
                nc.tensor.matmul(KF[:, :], k["w3k"][:, :], xt[:, slot % 2, :], start=True, stop=True).then_inc(s["kk"], 1)

            def vals(n, slot):
                need(pe, s["qt"], n + 1)
                for g in range(NG):
                    ins = nc.tensor.matmul(QV[:, g * D:(g + 1) * D], xt[:, slot % 2, g * N:(g + 1) * N], k["w3v"][:, :],
                                           start=True, stop=True)
                ins.then_inc(s["v"], 1)

            def norms(n, slot):
                need(pe, s["q2"], n + 1)
                need(pe, s["k2"], n + 1)
                need(pe, s["y_out"], n - 1)
                nc.tensor.matmul(KF[:, :], k["headsum"][:, :], q2[:, slot % 2, :], start=True, stop=False)
                nc.tensor.matmul(KF[:, :], k["headsum"][:, :], k2[:, slot % 2, :], start=False, stop=True).then_inc(s["f"], 1)

            def bound_row(n, slot):
                need(pe, s["fm"], n + 1)
                need(pe, s["on"], 2 * n)
                nc.tensor.matmul(f_row, fm[:, slot % 2:slot % 2 + 1], k["ident"][:, :], start=True, stop=True).then_inc(s["frow"], 1)

            def bound_all(n, slot):
                need(pe, s["f1"], n + 1)
                nc.tensor.matmul(f_all, k["onesf"][0:1, :], f1[0:1, slot % 2:slot % 2 + 1], start=True, stop=True).then_inc(s["fall"], 1)

            def scores(n, h, slot):
                need(pe, s["qt"], n + 1)
                need(pe, s["kt"], n + 1)
                need(pe, s["p"], H * (n - 1) + h + 1)
                r = slice(h * E, (h + 1) * E)
                for g in range(NG):
                    c = slice(g * N, (g + 1) * N)
                    ins = nc.tensor.matmul(S[h][:, c], kt[r, slot % 2, c], qt[r, slot % 2, c], start=True, stop=True)
                ins.then_inc(s["s"], 1)

            def attend(n, pair, slot):
                if pair == 0:
                    need(pe, s["pm"], (H - POOLED) * (n + 1))
                    need(pe, s["pmp"], POOLED * (n + 1))
                    need(pe, s["va"], n + 1)
                need(pe, s["on"], 2 * n + pair)
                for gg in range(2):
                    g = 2 * pair + gg
                    for h in range(H):
                        at = (gg * H + h) * w
                        ins = nc.tensor.matmul(O[:, at:at + w], pp[:, slot % 2, h, g * N:(g + 1) * N], va[:, slot % 2, g, h, :],
                                               start=True, stop=True)
                ins.then_inc(s["o"], 1)

            def transpose_on(n, slot):
                need(pe, s["on"], 2 * n + 2)
                need(pe, s["ont"], n)
                need(pe, s["xt"], min(n + 3, T) if known(n) else n + 3)
                for g in range(NG):
                    ins = nc.tensor.transpose(PT[:, g * N:(g + 1) * N], on[:, slot % 2, g, :], k["ident"][:, :])
                ins.then_inc(s["ont_tr"], 1)

            def project(n, slot):
                need(pe, s["ont"], n + 1)
                for g in range(NG):
                    out = KF[:, g * D:(g + 1) * D]
                    nc.tensor.matmul(out, k["ones96"][:, :], k["bias3"][:, :], start=True, stop=False, skip_group_check=True)
                    ins = nc.tensor.matmul(out, ont[:, g * N:(g + 1) * N], k["w3ot"][:, :], start=False, stop=True, skip_group_check=True)
                ins.then_inc(s["w"], 1)

            transpose_x(0, 0)
            queries(0, 0)
            keys(0, 0)
            vals(0, 0)
            transpose_x(1, 1)
            norms(0, 0)

            def step(t, slot, lap):
                a0, a1, c0 = (slot + 2) % RING, (slot + 1) % RING, (slot - 1) % RING
                in0 = not known(t) or t + 2 < T
                in1 = not known(t) or t + 1 < T
                inc = not known(t) or t >= 1
                scores(t, 0, slot)
                bound_row(t, slot)
                scores(t, 1, slot)
                bound_all(t, slot)
                if inc:
                    transpose_on(t - 1, c0)
                if in1:
                    queries(t + 1, a1)
                scores(t, 2, slot)
                if in1:
                    keys(t + 1, a1)
                scores(t, 3, slot)
                if in1:
                    vals(t + 1, a1)
                if inc:
                    need(pe, s["kt"], t + 1) if not in1 else need(pe, s["kt"], t + 2)
                    project(t - 1, c0)
                if in0:
                    transpose_x(t + 2, a0)
                attend(t, 0, slot)
                if in1:
                    norms(t + 1, a1)
                attend(t, 1, slot)

            steps(pe, step)
            need(pe, s["on"], 2 * T)
            transpose_on(T - 1, (T - 1) % RING)
            project(T - 1, (T - 1) % RING)


def write_out(nc, sb, sem, yres, mean, rstd, out_ngd):
    xo = sb("xo", [N, RING, NG, D], F32)
    s = {n: sem(f"out_{n}") for n in ("ln",)}
    out_done = [sem(f"out_done{r}") for r in range(RING)]
    with nc.Block() as block:
        @block.vector
        def _(dve):
            for n in range(RING):
                normalized(nc, dve, s, xo, yres, mean, rstd, n, n)
            with dve.Fori(1, T // RING) as i:
                for r in range(RING):
                    dve.wait_ge(out_done[r], 16 * i)
                    normalized(nc, dve, s, xo, yres, mean, rstd, i * RING + r, r)

        @block.sync
        def _(sp):
            with sp.Fori(0, T // RING) as i:
                for r in range(RING):
                    sp.wait_ge(s["ln"], i * RING + r + 1)
                    sp.dma_start(out_ngd[:, bass.ds((i * RING + r) * NG, NG), :], xo[:, r, :, :]).then_inc(out_done[r], 16)
            for r in range(RING):
                sp.wait_ge(out_done[r], 16 * (T // RING))


class General:

    def __init__(self, nc, sb, pb, k, c, out_ngd):
        self.nc, self.pb, self.k, self.c, self.out = nc, pb, k, c, out_ngd
        self.adji = sb("g_adji", [N, N], I32)
        self.adjti = sb("g_adjti", [N, N], I32)
        self.adjf = sb("g_adjf", [N, N], F32)
        self.adjtf = sb("g_adjtf", [N, N], F32)
        self.x = sb("g_x", [N, D], F32)
        self.xt = sb("g_xt", [D, N], F32)
        self.y = sb("g_y", [N, D], F32)
        self.mask = sb("g_mask", [N, N], F32)
        self.fill = sb("g_fill", [N, N], F32)
        self.wh = sb("g_wh", [N, D], F32)
        self.qt = sb("g_qt", [D, N], F32)
        self.kt = sb("g_kt", [D, N], F32)
        self.e = sb("g_e", [N, N], F32)
        self.e2 = sb("g_e2", [N, N], F32)
        self.pt = sb("g_pt", [N, N], F32)
        self.small = sb("g_small", [N, 4], F32)
        self.bn = sb("g_bn", [N, 8], F32)
        self.eps = sb("g_eps", [N, 1], F32)
        self.wide = sb("g_wide", [D, 18, N], F32)
        self.wdir = sb("g_wdir", [D, 2, 2 * D], F32)
        self.hg = sb("g_hg", [N, 2, 2 * D], F32)
        self.brows = sb("g_brows", [1, 39 * 4 * D], F32)
        self.rels = sb("g_rels", [N, 39], F32)
        self.onehot = sb("g_onehot", [N, 2, N], F32)
        self.val = sb("g_val", [N, 2, 2 * D], F32)

    def sems(self, sem, stage):
        self.own, self.operands, self.product, self.arguments, self.activated, self.loaded, self.stored = (
            sem(f"{stage}_{n}") for n in "own operands product arguments activated loaded stored".split())
        self.counts = dict.fromkeys(("own", "product", "activated"), 0)

    def link(self, ins):
        self.counts["own"] += 1
        ins.then_inc(self.own, 1)
        self.nc.vector.wait_ge(self.own, self.counts["own"])

    def by_pe(self, ins):
        self.counts["product"] += 1
        ins.then_inc(self.operands, 1)
        self.nc.vector.wait_ge(self.product, self.counts["product"])

    def by_act(self, ins):
        self.counts["activated"] += 1
        ins.then_inc(self.arguments, 1)
        self.nc.vector.wait_ge(self.activated, self.counts["activated"])

    def prepare(self, nc, tsb, sem):
        k, c = self.k, self.c
        self.sems(sem, "prepare")
        w, wt, wgt = (tsb(n, [D, 2, D], F32) for n in ("g_w", "g_wt", "g_wgt"))
        with nc.Block() as block:
            @block.sync
            def _(sp):
                for e, name in enumerate(("f", "b")):
                    for dst, src in ((w, "w"), (wt, "wt"), (wgt, "wgt")):
                        sp.dma_start(dst[:, e, :], c[f"{src}_{name}"]).then_inc(self.loaded, 16)
                sp.dma_start(self.brows[:, :], c["brows"]).then_inc(self.loaded, 16)
                sp.dma_start(self.rels[:, :], c["rels"]).then_inc(self.loaded, 16)

            @block.vector
            def _(dve):
                nc.vector.memset(self.eps[:, :], EPS)
                for n in range(18):
                    src = k["wa0"][:, n:n + 1] if n < 16 else k["wa1"][:, n - 16:n - 15]
                    nc.vector.tensor_copy(self.wide[:, n, :], src.to_broadcast([D, N]))
                dve.wait_ge(self.loaded, 16 * 8)
                self.by_pe(nc.vector.tensor_copy(self.wdir[:, :, 0:D], wt[:, :, :]))
                nc.vector.tensor_copy(self.wdir[:, :, D:2 * D], self.pb[0][:, 0:2 * D].rearrange("p (e d) -> p e d", e=2))

            @block.tensor
            def _(pe):
                pe.wait_ge(self.operands, 1)
                for e in range(2):
                    ins = nc.tensor.matmul(self.pb[0][:, e * D:(e + 1) * D], w[:, e, :], wgt[:, e, :], start=True, stop=True)
                ins.then_inc(self.product, 1)


    def dve_edges(self, dve, op, value):
        nc = self.nc
        self.link(nc.vector.tensor_scalar(self.mask[:, :], self.adjf[:, :], value, None, op))
        self.link(nc.vector.tensor_scalar(self.fill[:, :], self.mask[:, :], -1.0, 3e38, ALU.add, ALU.mult))

    def dve_softmax(self, dve, scores, slope, scale):
        nc, e, e2, sm = self.nc, self.e, self.e2, self.small
        self.link(nc.vector.tensor_scalar(e[:, :], scores, scale, None, ALU.mult))
        if slope is not None:
            self.link(nc.vector.scalar_tensor_tensor(e[:, :], e[:, :], slope, e[:, :], ALU.mult, ALU.max))
        self.link(nc.vector.tensor_tensor(e[:, :], e[:, :], self.mask[:, :], ALU.mult))
        self.link(nc.vector.tensor_tensor(e[:, :], e[:, :], self.fill[:, :], ALU.add))
        self.link(nc.vector.reduce_max(sm[:, 0:1], e[:, :], AX_X))
        self.by_act(nc.vector.tensor_scalar(e[:, :], e[:, :], sm[:, 0:1], None, ALU.subtract))
        self.link(nc.vector.tensor_tensor(e2[:, :], e2[:, :], self.mask[:, :], ALU.mult))
        self.link(nc.vector.reduce_sum(sm[:, 1:2], e2[:, :], AX_X))
        self.link(nc.vector.reciprocal(sm[:, 2:3], sm[:, 1:2]))
        self.by_pe(nc.vector.tensor_scalar(e2[:, :], e2[:, :], sm[:, 2:3], None, ALU.mult))
        self.by_pe(nc.vector.tensor_copy(self.pt[:, :], self.pb[2][:, 0:N]))

    def dve_norm(self, dve):
        nc, bn = self.nc, self.bn
        self.link(nc.vector.bn_stats(bn[:, 0:6], self.y[:, :]))
        self.link(nc.vector.bn_aggr(self.small[:, 0:2], bn[:, 0:6]))
        self.by_act(nc.vector.tensor_scalar(bn[:, 6:7], self.small[:, 1:2], EPS, None, ALU.add))
        self.link(nc.vector.reciprocal(self.small[:, 2:3], bn[:, 7:8]))
        self.by_pe(nc.vector.tensor_scalar(self.x[:, :], self.y[:, :], self.small[:, 0:1], self.small[:, 2:3],
                                           ALU.subtract, ALU.mult))

    def dve_xt(self, dve):
        self.by_pe(self.nc.vector.tensor_copy(self.xt[:, :], self.pb[0][:, 0:N]))


    def pe_take(self, pe):
        self.taken += 1
        pe.wait_ge(self.operands, self.taken)

    def pe_give(self, ins):
        ins.then_inc(self.product, 1)

    def pe_softmax(self, pe, values, out):
        nc = self.nc
        self.pe_take(pe)
        self.pe_give(nc.tensor.transpose(self.pb[2][:, 0:N], self.e2[:, :], self.k["ident"][:, :]))
        self.pe_take(pe)
        self.pe_give(nc.tensor.matmul(out, self.pt[:, :], values, start=True, stop=True))

    def pe_transpose(self, pe, src):
        self.pe_take(pe)
        self.pe_give(self.nc.tensor.transpose(self.pb[0][:, 0:N], src[:, :], self.k["ident"][:, :]))

    def act_take(self, act):
        self.acted += 1
        act.wait_ge(self.arguments, self.acted)

    def act_softmax(self, act):
        self.act_take(act)
        self.nc.scalar.activation(self.e2[:, :], self.e[:, :], ACT.Exp).then_inc(self.activated, 1)

    def act_norm(self, act):
        self.act_take(act)
        self.nc.scalar.activation(self.bn[:, 7:8], self.bn[:, 6:7], ACT.Sqrt).then_inc(self.activated, 1)

    def front(self, nc, tsb, sem, g):
        k, c, pb = self.k, self.c, self.pb
        self.sems(sem, "front")
        self.taken = self.acted = 0
        layers = ((8, 16, 0, k["w0"]), (1, 128, 16, k["w1t"]))

        with nc.Block() as block:
            @block.sync
            def _(sp):
                for dst, src in ((self.adji, c["adj"]), (self.adjti, c["adjt"]), (self.x, c["x"]), (self.xt, c["xt"])):
                    sp.dma_start(dst[:, :], src[:, bass.ds(g, 1), :].rearrange("p o n -> p (o n)")).then_inc(self.loaded, 16)

            @block.vector
            def _(dve):
                dve.wait_ge(self.loaded, 64)
                nc.vector.tensor_copy(self.adjtf[:, :], self.adjti[:, :])
                self.link(nc.vector.tensor_copy(self.adjf[:, :], self.adji[:, :]))
                self.dve_edges(dve, ALU.not_equal, 0.0)
                for H, hd, at, _ in layers:
                    if H == 1:
                        self.dve_xt(dve)
                    else:
                        self.by_pe(nc.vector.tensor_copy(self.y[:, :], self.x[:, :]))
                    for h in range(H):
                        self.by_pe(nc.vector.tensor_copy(self.wh[:, :], pb[1][:, 0:D]) if h == 0 else
                                   nc.vector.tensor_copy(self.y[:, (h - 1) * hd:h * hd], pb[3][:, 0:hd]))
                        self.dve_softmax(dve, pb[0][:, 0:N], 0.2, 1.0)
                    self.link(nc.vector.tensor_copy(self.y[:, (H - 1) * hd:H * hd], pb[3][:, 0:hd]))
                    if H == 1:
                        self.by_act(nc.vector.tensor_scalar(self.e[:, :], self.y[:, :], 0.0, None, ALU.min))
                        self.link(nc.vector.scalar_tensor_tensor(self.y[:, :], self.y[:, :], 0.0, self.e2[:, :], ALU.max, ALU.add))
                        self.link(nc.vector.scalar_tensor_tensor(self.y[:, :], self.y[:, :], -1.0, self.x[:, :], ALU.add, ALU.add))
                    else:
                        self.link(nc.vector.tensor_tensor(self.y[:, :], self.y[:, :], self.x[:, :], ALU.add))
                    self.dve_norm(dve)
                self.dve_xt(dve)
                nc.vector.tensor_copy(self.hg[:, :, :], pb[1][:, :].rearrange("p (e d) -> p e d", e=2))
                self.link(nc.vector.tensor_scalar(self.onehot[:, 0, :], self.adjf[:, :], 1.0, None, ALU.is_equal))
                self.by_act(nc.vector.tensor_copy(self.val[:, 0, :], pb[3][:, 0:2 * D]))
                self.by_pe(nc.vector.scalar_tensor_tensor(self.val[:, 1, 0:D], self.e[:, :], 1.0, self.val[:, 0, 0:D],
                                                          ALU.add, ALU.mult))

            @block.scalar
            def _(act):
                for H, hd, at, _ in layers:
                    for h in range(H):
                        self.act_softmax(act)
                    if H == 1:
                        self.act_softmax(act)
                    self.act_norm(act)
                self.act_take(act)
                nc.scalar.activation(self.e[:, :], self.val[:, 0, D:2 * D], ACT.Tanh, scale=0.5).then_inc(self.activated, 1)

            @block.tensor
            def _(pe):
                for H, hd, at, wm in layers:
                    self.pe_take(pe)
                    self.pe_give(nc.tensor.matmul(pb[1][:, 0:D], self.xt[:, :], wm[:, :], start=True, stop=True))
                    for h in range(H):
                        self.pe_take(pe)
                        nc.tensor.matmul(pb[0][:, 0:N], self.xt[:, :], self.wide[:, at + h, :], start=True, stop=False)
                        self.pe_give(nc.tensor.matmul(pb[0][:, 0:N], self.wide[:, at + H + h, :], self.xt[:, :], start=False, stop=True))
                        self.pe_softmax(pe, self.wh[:, h * hd:(h + 1) * hd], pb[3][:, 0:hd])
                    self.pe_transpose(pe, self.x)
                self.pe_take(pe)
                nc.tensor.matmul(pb[3][:, 0:2 * D], k["ones96"][:, :], k["bias2"][:, :], start=True, stop=False, skip_group_check=True)
                nc.tensor.matmul(pb[3][:, 0:2 * D], self.xt[:, :], k["w2"][:, :], start=False, stop=True, skip_group_check=True)
                self.pe_give(nc.tensor.matmul(pb[1][:, :], self.xt[:, :], self.wdir[:, :, :].rearrange("d e o -> d (e o)"),
                                              start=True, stop=True))
                self.pe_take(pe)
                self.pe_give(nc.tensor.matmul(pb[4][:, 0:D], self.onehot[:, 0, :], self.val[:, 1, 0:D], start=True, stop=False,
                                              skip_group_check=True))

    def relation(self, nc, tsb, sem, r):
        pb = self.pb
        self.sems(sem, "relation")
        with nc.Block() as block:
            @block.vector
            def _(dve):
                nc.vector.tensor_scalar(self.onehot[:, 0, :], self.adjtf[:, :], self.rels[:, bass.ds(r, 1)], None, ALU.is_equal)
                nc.vector.tensor_scalar(self.onehot[:, 1, :], self.adjf[:, :], self.rels[:, bass.ds(r, 1)], None, ALU.is_equal)
                dve.wait_ge(self.product, 1)
                self.by_act(nc.vector.tensor_tensor(self.val[:, :, :], self.hg[:, :, :], pb[5][:, :].rearrange("p (e d) -> p e d", e=2), ALU.add))
                self.link(nc.vector.tensor_scalar(self.val[:, :, D:2 * D], self.val[:, :, D:2 * D], 0.5, 0.5, ALU.mult, ALU.add))
                nc.vector.tensor_tensor(self.val[:, :, 0:D], self.val[:, :, 0:D], self.val[:, :, D:2 * D], ALU.mult).then_inc(self.operands, 1)

            @block.scalar
            def _(act):
                act.wait_ge(self.arguments, 1)
                v = self.val[:, :, D:2 * D]
                nc.scalar.activation(v, v, ACT.Tanh, scale=0.5).then_inc(self.activated, 1)

            @block.tensor
            def _(pe):
                nc.tensor.matmul(pb[5][:, :], self.k["onesf"][0:1, :], self.brows[0:1, bass.ds(r * (4 * D), 4 * D)],
                                 start=True, stop=True).then_inc(self.product, 1)
                pe.wait_ge(self.operands, 1)
                for e in range(2):
                    nc.tensor.matmul(pb[4][:, 0:D], self.onehot[:, e, :], self.val[:, e, 0:D], start=False, stop=False,
                                     skip_group_check=True)

    def back(self, nc, tsb, sem, g):
        k, pb = self.k, self.pb
        self.sems(sem, "back")
        self.taken = self.acted = 0
        H, E = 4, 32
        with nc.Block() as block:
            @block.vector
            def _(dve):
                self.link(nc.vector.tensor_scalar(self.y[:, :], pb[4][:, 0:D], 0.0, None, ALU.max))
                self.link(nc.vector.tensor_tensor(self.y[:, :], self.y[:, :], self.x[:, :], ALU.add))
                self.dve_norm(dve)
                self.dve_edges(dve, ALU.is_gt, 0.0)
                self.dve_xt(dve)
                nc.vector.tensor_copy(self.qt[:, :], pb[1][:, 0:N])
                nc.vector.tensor_copy(self.kt[:, :], pb[1][:, N:2 * N])
                for h in range(H):
                    self.by_pe(nc.vector.tensor_copy(self.wh[:, :], pb[1][:, 2 * N:3 * N]) if h == 0 else
                               nc.vector.tensor_copy(self.y[:, (h - 1) * E:h * E], pb[3][:, 0:E]))
                    self.dve_softmax(dve, pb[0][:, 0:N], None, E ** -0.5)
                self.by_pe(nc.vector.tensor_copy(self.y[:, (H - 1) * E:H * E], pb[3][:, 0:E]))
                self.by_pe(nc.vector.tensor_copy(self.xt[:, :], pb[0][:, 0:N]))
                self.link(nc.vector.tensor_tensor(self.y[:, :], pb[3][:, 0:D], self.x[:, :], ALU.add))
                self.dve_norm(dve)

            @block.scalar
            def _(act):
                self.act_norm(act)
                for h in range(H):
                    self.act_softmax(act)
                self.act_norm(act)

            @block.tensor
            def _(pe):
                self.pe_transpose(pe, self.x)
                self.pe_take(pe)
                nc.tensor.matmul(pb[1][:, 0:N], k["w3q"][:, :], self.xt[:, :], start=True, stop=True)
                nc.tensor.matmul(pb[1][:, N:2 * N], k["w3k"][:, :], self.xt[:, :], start=True, stop=True)
                self.pe_give(nc.tensor.matmul(pb[1][:, 2 * N:3 * N], self.xt[:, :], k["w3v"][:, :], start=True, stop=True))
                for h in range(H):
                    r = slice(h * E, (h + 1) * E)
                    self.pe_take(pe)
                    self.pe_give(nc.tensor.matmul(pb[0][:, 0:N], self.qt[r, :], self.kt[r, :], start=True, stop=True))
                    self.pe_softmax(pe, self.wh[:, r], pb[3][:, 0:E])
                self.pe_transpose(pe, self.y)
                self.pe_take(pe)
                nc.tensor.matmul(pb[3][:, 0:D], k["ones96"][:, :], k["bias3"][:, :], start=True, stop=False, skip_group_check=True)
                self.pe_give(nc.tensor.matmul(pb[3][:, 0:D], self.xt[:, :], k["w3ot"][:, :], start=False, stop=True, skip_group_check=True))
                self.pe_transpose(pe, self.x)

            @block.sync
            def _(sp):
                sp.wait_ge(self.operands, 3 * H + 5)
                sp.dma_start(self.out[:, bass.ds(g, 1), :].rearrange("p o d -> p (o d)"), self.x[:, :]).then_inc(self.stored, 16)
                sp.wait_ge(self.stored, 16)


def verdict(nc, sb, sem, pb, k, dmin, adjbad, flag):
    s = {n: sem(f"flag_{n}") for n in ("own", "col", "row")}
    col = sb("flag_col", [N, 4], F32)
    row = sb("flag_row", [1, 1], F32)
    with nc.Block() as block:
        @block.vector
        def _(dve):
            nc.vector.tensor_reduce(col[:, 0:1], dmin[:, :], AX_X, ALU.min).then_inc(s["own"], 1)
            nc.vector.reduce_max(col[:, 1:2], adjbad[:, :], AX_X).then_inc(s["own"], 1)
            dve.wait_ge(s["own"], 2)
            nc.vector.tensor_scalar(col[:, 2:3], col[:, 0:1], 1e-28, None, ALU.is_ge).then_inc(s["own"], 1)
            nc.vector.tensor_scalar(col[:, 3:4], col[:, 1:2], NG * N / 4, None, ALU.is_le).then_inc(s["own"], 1)
            dve.wait_ge(s["own"], 4)
            nc.vector.tensor_tensor(col[:, 0:1], col[:, 2:3], col[:, 3:4], ALU.mult).then_inc(s["col"], 1)
            dve.wait_ge(s["row"], 1)
            nc.vector.tensor_copy(row[:, :], pb[0][0:1, 0:1]).then_inc(s["own"], 1)
            dve.wait_ge(s["own"], 5)
            nc.vector.tensor_scalar(flag[:, :], row[:, :], float(N), None, ALU.is_lt)

        @block.tensor
        def _(pe):
            pe.wait_ge(s["col"], 1)
            nc.tensor.matmul(pb[0][0:1, 0:1], col[:, 0:1], k["onescol"][:, :], start=True, stop=True).then_inc(s["row"], 1)



class Banks:

    def __init__(self, ctx, nc):
        self.all = ctx.enter_context(nc.psum_tensor("banks", [N, 8 * BANK], F32))

    def __getitem__(self, n):
        return self.all[:, n * BANK:(n + 1) * BANK]

    def pair(self, n):
        return self.all[:, n * BANK:(n + 2) * BANK]


def build(nc, c, out_ngd):
    with ExitStack() as ctx:
        def sb(name, shape, dt):
            return ctx.enter_context(nc.sbuf_tensor(name, shape, dt))

        pb = Banks(ctx, nc)
        flag = sb("flag", [1, 1], I32)
        stats = sb("stats", [N, B, 6], F32)
        mean = sb("mean", [N, B], F32)
        rstd = sb("rstd", [N, B], F32)
        dmin = sb("dmin", [N, 32], F32)
        adjbad = sb("adjbad", [N, T], F32)
        k = {}

        def phase(f, *args):
            sems = []

            def sem(name):
                sems.append(nc.alloc_semaphore(name=name))
                return sems[-1]

            with ExitStack() as own:
                f(nc, lambda name, shape, dt: own.enter_context(nc.sbuf_tensor(name, shape, dt)), sem, *args)
            nc.clear_and_free_semaphores(sems)
            nc.all_engine_barrier()

        phase(constants, sb, pb, c, k)

        fast = ExitStack()
        yres = fast.enter_context(nc.sbuf_tensor("yres", [N, B, D], F32))
        phase(gat, pb, k, 0, 8, yres, stats, mean, rstd, dmin, c["x"], c["xt"], c["adjt"])
        phase(row_statistics, 0, stats, mean, rstd)
        phase(gat, pb, k, 1, 1, yres, stats, mean, rstd, dmin, c["x"], c["xt"], c["adjt"])
        phase(row_statistics, 1, stats, mean, rstd)
        phase(relational, pb, k, yres, stats, mean, rstd, adjbad, c["adj"])
        phase(row_statistics, 2, stats, mean, rstd)
        phase(heads, pb, k, yres, stats, mean, rstd, dmin, c["adjt"])
        phase(row_statistics, 3, stats, mean, rstd)
        phase(write_out, yres, mean, rstd, out_ngd)
        phase(verdict, pb, k, dmin, adjbad, flag)
        fast.close()

        some = nc.values_load(flag[0:1, 0:1], min_val=0, max_val=1)
        with nc.If(some > 0):
            nc.all_engine_barrier()
            general = General(nc, sb, pb, k, c, out_ngd)
            phase(general.prepare)
            with nc.Fori(0, B) as g:
                phase(general.front, g)
                with nc.Fori(0, 39) as r:
                    phase(general.relation, r)
                phase(general.back, g)


def kernel(**inputs):
    import numpy as np
    import concourse.bacc as bacc
    from concourse.bass_utils import run_bass_kernel_spmd

    i = {n: np.asarray(a) for n, a in inputs.items()}
    eye = np.eye(32, dtype=np.float32)
    lay = {
        "x": i["x"].transpose(1, 0, 2),
        "xt": i["x"].transpose(2, 0, 1),
        "adj": i["adj"].transpose(1, 0, 2),
        "adjt": i["adj"].transpose(2, 0, 1),
        "w0": i["L0_gnn_W"], "w0t": i["L0_gnn_W"].T,
        "a0": np.concatenate([i["L0_gnn_a"].reshape(2, 16).T] * 8, axis=0),
        "w1": i["L1_gnn_W"], "w1t": i["L1_gnn_W"].T, "a1": i["L1_gnn_a"].reshape(2, D).T,
        "wl": i["L2_gnn_W_loop"], "wlt": i["L2_gnn_W_loop"].T, "wgt": i["L2_gnn_Wg_loop"].T,
        "b2": i["L2_gnn_b_loop"], "bg2": i["L2_gnn_bg_loop"],
        "wq": i["L3_gnn_Wq"].transpose(1, 0, 2).reshape(D, D), "wk": i["L3_gnn_Wk"].transpose(1, 0, 2).reshape(D, D),
        "wv": i["L3_gnn_Wv"].transpose(1, 0, 2).reshape(D, D), "wot": i["L3_gnn_Wo"].T, "bo": i["L3_gnn_bo"].reshape(1, D),
        "w_f": i["L2_gnn_W_fwd"], "wt_f": i["L2_gnn_W_fwd"].T, "wgt_f": i["L2_gnn_Wg_fwd"].T,
        "w_b": i["L2_gnn_W_bwd"], "wt_b": i["L2_gnn_W_bwd"].T, "wgt_b": i["L2_gnn_Wg_bwd"].T,
        "brows": np.concatenate([i[f"L2_gnn_{n}"] for n in ("b_fwd", "bg_fwd", "b_bwd", "bg_bwd")], axis=1).reshape(1, 39 * 4 * D),
        "rels": np.broadcast_to(np.arange(2, 41, dtype=np.float32), (N, 39)),
        "ident": np.eye(N, dtype=np.float32), "eye3": np.concatenate([eye] * 3, axis=0),
        "hb": np.repeat(np.eye(8, dtype=np.float32), 16, axis=0),
        "headsum": np.repeat(np.repeat(np.eye(4, dtype=np.float32), 32, axis=0), 32, axis=1),
    }
    nc = bacc.Bacc("TRN2", target_bir_lowering=False, num_devices=1)
    arrays, c = {}, {}
    for name, a in lay.items():
        arrays[f"in_{name}"] = np.ascontiguousarray(a)
        c[name] = nc.dram_tensor(f"in_{name}", a.shape, mybir.dt.from_np(a.dtype), kind="ExternalInput").ap()
    out = nc.dram_tensor("out_ngd", (N, B, D), F32, kind="ExternalOutput").ap()
    build(nc, c, out)
    r = run_bass_kernel_spmd(nc, [arrays], core_ids=[0])
    return r.results[0]["out_ngd"].transpose(1, 0, 2)
```
